# Optimizing a Trainium2 kernel written in Bass

```python
import numpy as np
import jax
import jax.numpy as jnp

def _softmax(x, axis=-1):
    return jax.nn.softmax(x, axis=axis)

def _gelu(x):
    return jax.nn.gelu(x, approximate=True)

def _silu(x):
    return jax.nn.silu(x)

def _sigmoid(x):
    return jax.nn.sigmoid(x)

def _layernorm(x, axis=-1, eps=1e-05):
    m = jnp.mean(x, axis=axis, keepdims=True)
    v = jnp.var(x, axis=axis, keepdims=True)
    return (x - m) / jnp.sqrt(v + eps)

def _scatter_add(tgt, idx, src, axis=0):
    return tgt.at[idx].add(src)

def _segment_sum(src, seg, n):
    return jax.ops.segment_sum(src, seg, n)
kernel_name = 'mk_cond_resid_d4_seqx_r2_229f4d'

def setup_inputs(seed: int=0):
    np.random.seed(seed)
    _w = jnp.asarray

    def _rec_inputs():
        import jax
        import jax.numpy as jnp
        _rk = jax.random.key(seed)
        x = -0.0003929 + 0.9999 * jax.random.normal(jax.random.fold_in(_rk, 1), (32, 128, 512), jnp.float32)
        _lenS = 128 - jax.random.randint(jax.random.fold_in(_rk, 7), (32,), 0, max(1, 128 // 4) + 1, jnp.int32)
        _lenS2 = 128 - jax.random.randint(jax.random.fold_in(_rk, 8), (32,), 0, max(1, 128 // 4) + 1, jnp.int32)
        cond_2048 = 0.00782532 + 1.00527 * jax.random.normal(jax.random.fold_in(_rk, 11), (32, 1024), jnp.float32)
        return (x, cond_2048)
    x, cond_2048 = _rec_inputs()

    def _L0_cond_setup():
        import jax, jax.numpy as jnp
        import numpy as np
        B, S, D_MODEL, D_INNER, D_STATE = (4, 2048, 512, 1024, 16)
        key = jax.random.key(seed)
        ks = jax.random.split(key, 12)
        inp = {'x': jax.random.normal(ks[0], (B, S, D_MODEL), jnp.float32), 't_emb': jax.random.normal(ks[1], (B, D_INNER), jnp.float32), 'W_in': jax.random.normal(ks[2], (2 * D_INNER, D_MODEL), jnp.float32) * 0.02, 'W_conv': jax.random.normal(ks[3], (D_INNER, 1, 4), jnp.float32) * 0.1, 'b_conv': jnp.zeros((D_INNER,), jnp.float32), 'ln_g': jnp.ones((D_INNER,), jnp.float32), 'ln_b': jnp.zeros((D_INNER,), jnp.float32), 'W_xproj': jax.random.normal(ks[4], (3 * D_STATE, D_INNER), jnp.float32) * 0.02, 'W_dt': jax.random.normal(ks[5], (D_STATE, D_STATE), jnp.float32) * 0.01, 'b_dt': jax.random.uniform(ks[6], (D_STATE,), jnp.float32) * 0.1, 'A_log': jax.random.normal(ks[7], (D_STATE,), jnp.float32) * 0.1, 'D': jnp.ones((D_INNER,), jnp.float32) * 0.1, 'W_out': jax.random.normal(ks[8], (D_MODEL, D_INNER), jnp.float32) * 0.02}
        return inp
    _L0_cond_all = _L0_cond_setup()
    _L0_cond_in = {k: v for k, v in _L0_cond_all.items() if k in ('W_in', 'W_conv', 'b_conv', 'ln_g', 'ln_b', 'W_xproj', 'W_dt', 'b_dt', 'A_log', 'D', 'W_out')}
    del _L0_cond_all

    def _L1_cond_setup():
        import jax, jax.numpy as jnp
        import numpy as np
        EPS_IN = 1e-05
        EPS_DM = 1e-08

        def _dcoef(weight, style):
            return jax.lax.rsqrt(jnp.einsum('oi,bi->bo', jnp.square(weight), jnp.square(style)) + EPS_DM)
        key = jax.random.key(seed)
        ks = jax.random.split(key, 7)
        B, S, H = (8, 512, 512)
        lim = 1.0 / np.sqrt(H)
        u = lambda k, shp: jax.random.uniform(k, shp, jnp.float32, -lim, lim)
        return {'x': jax.random.normal(ks[0], (B, S, H), jnp.float32), 'q_weight': u(ks[1], (H, H)), 'k_weight': u(ks[2], (H, H)), 'v_weight': u(ks[3], (H, H)), 'w_weight': u(ks[4], (H, H)), 'u_weight': u(ks[5], (H, H)), 'styles': jax.random.normal(ks[6], (B, 2 * H), jnp.float32) * 0.5 + 1.0, 'num_heads': 16}
    _L1_cond_all = _L1_cond_setup()
    _L1_cond_in = {k: v for k, v in _L1_cond_all.items() if k in ('q_weight', 'k_weight', 'v_weight', 'w_weight', 'u_weight')}
    del _L1_cond_all

    def _L2_cond_setup():
        import jax, jax.numpy as jnp
        import numpy as np
        EPS_IN = 1e-05
        EPS_DM = 1e-08

        def _dcoef(weight, style):
            return jax.lax.rsqrt(jnp.einsum('oi,bi->bo', jnp.square(weight), jnp.square(style)) + EPS_DM)
        key = jax.random.key(seed)
        ks = jax.random.split(key, 7)
        B, S, H = (8, 512, 512)
        lim = 1.0 / np.sqrt(H)
        u = lambda k, shp: jax.random.uniform(k, shp, jnp.float32, -lim, lim)
        return {'x': jax.random.normal(ks[0], (B, S, H), jnp.float32), 'q_weight': u(ks[1], (H, H)), 'k_weight': u(ks[2], (H, H)), 'v_weight': u(ks[3], (H, H)), 'w_weight': u(ks[4], (H, H)), 'u_weight': u(ks[5], (H, H)), 'styles': jax.random.normal(ks[6], (B, 2 * H), jnp.float32) * 0.5 + 1.0, 'num_heads': 16}
    _L2_cond_all = _L2_cond_setup()
    _L2_cond_in = {k: v for k, v in _L2_cond_all.items() if k in ('q_weight', 'k_weight', 'v_weight', 'w_weight', 'u_weight')}
    del _L2_cond_all

    def _L3_cond_setup():
        import jax, jax.numpy as jnp
        import numpy as np
        B, S, D_MODEL, D_INNER, D_STATE = (4, 2048, 512, 1024, 16)
        key = jax.random.key(seed)
        ks = jax.random.split(key, 12)
        inp = {'x': jax.random.normal(ks[0], (B, S, D_MODEL), jnp.float32), 't_emb': jax.random.normal(ks[1], (B, D_INNER), jnp.float32), 'W_in': jax.random.normal(ks[2], (2 * D_INNER, D_MODEL), jnp.float32) * 0.02, 'W_conv': jax.random.normal(ks[3], (D_INNER, 1, 4), jnp.float32) * 0.1, 'b_conv': jnp.zeros((D_INNER,), jnp.float32), 'ln_g': jnp.ones((D_INNER,), jnp.float32), 'ln_b': jnp.zeros((D_INNER,), jnp.float32), 'W_xproj': jax.random.normal(ks[4], (3 * D_STATE, D_INNER), jnp.float32) * 0.02, 'W_dt': jax.random.normal(ks[5], (D_STATE, D_STATE), jnp.float32) * 0.01, 'b_dt': jax.random.uniform(ks[6], (D_STATE,), jnp.float32) * 0.1, 'A_log': jax.random.normal(ks[7], (D_STATE,), jnp.float32) * 0.1, 'D': jnp.ones((D_INNER,), jnp.float32) * 0.1, 'W_out': jax.random.normal(ks[8], (D_MODEL, D_INNER), jnp.float32) * 0.02}
        return inp
    _L3_cond_all = _L3_cond_setup()
    _L3_cond_in = {k: v for k, v in _L3_cond_all.items() if k in ('W_in', 'W_conv', 'b_conv', 'ln_g', 'ln_b', 'W_xproj', 'W_dt', 'b_dt', 'A_log', 'D', 'W_out')}
    del _L3_cond_all
    return {'x': x, 'cond_2048': cond_2048, 'L0_cond_W_in': _L0_cond_in['W_in'], 'L0_cond_W_conv': _L0_cond_in['W_conv'], 'L0_cond_b_conv': _L0_cond_in['b_conv'], 'L0_cond_ln_g': _L0_cond_in['ln_g'], 'L0_cond_ln_b': _L0_cond_in['ln_b'], 'L0_cond_W_xproj': _L0_cond_in['W_xproj'], 'L0_cond_W_dt': _L0_cond_in['W_dt'], 'L0_cond_b_dt': _L0_cond_in['b_dt'], 'L0_cond_A_log': _L0_cond_in['A_log'], 'L0_cond_D': _L0_cond_in['D'], 'L0_cond_W_out': _L0_cond_in['W_out'], 'L1_cond_q_weight': _L1_cond_in['q_weight'], 'L1_cond_k_weight': _L1_cond_in['k_weight'], 'L1_cond_v_weight': _L1_cond_in['v_weight'], 'L1_cond_w_weight': _L1_cond_in['w_weight'], 'L1_cond_u_weight': _L1_cond_in['u_weight'], 'L2_cond_q_weight': _L2_cond_in['q_weight'], 'L2_cond_k_weight': _L2_cond_in['k_weight'], 'L2_cond_v_weight': _L2_cond_in['v_weight'], 'L2_cond_w_weight': _L2_cond_in['w_weight'], 'L2_cond_u_weight': _L2_cond_in['u_weight'], 'L3_cond_W_in': _L3_cond_in['W_in'], 'L3_cond_W_conv': _L3_cond_in['W_conv'], 'L3_cond_b_conv': _L3_cond_in['b_conv'], 'L3_cond_ln_g': _L3_cond_in['ln_g'], 'L3_cond_ln_b': _L3_cond_in['ln_b'], 'L3_cond_W_xproj': _L3_cond_in['W_xproj'], 'L3_cond_W_dt': _L3_cond_in['W_dt'], 'L3_cond_b_dt': _L3_cond_in['b_dt'], 'L3_cond_A_log': _L3_cond_in['A_log'], 'L3_cond_D': _L3_cond_in['D'], 'L3_cond_W_out': _L3_cond_in['W_out']}

def reference(x, cond_2048, L0_cond_W_in, L0_cond_W_conv, L0_cond_b_conv, L0_cond_ln_g, L0_cond_ln_b, L0_cond_W_xproj, L0_cond_W_dt, L0_cond_b_dt, L0_cond_A_log, L0_cond_D, L0_cond_W_out, L1_cond_q_weight, L1_cond_k_weight, L1_cond_v_weight, L1_cond_w_weight, L1_cond_u_weight, L2_cond_q_weight, L2_cond_k_weight, L2_cond_v_weight, L2_cond_w_weight, L2_cond_u_weight, L3_cond_W_in, L3_cond_W_conv, L3_cond_b_conv, L3_cond_ln_g, L3_cond_ln_b, L3_cond_W_xproj, L3_cond_W_dt, L3_cond_b_dt, L3_cond_A_log, L3_cond_D, L3_cond_W_out):
    import jax
    import jax.numpy as jnp

    def _L0_cond_ref(x, t_emb, W_in, W_conv, b_conv, ln_g, ln_b, W_xproj, W_dt, b_dt, A_log, D, W_out):
        import jax, jax.numpy as jnp
        import numpy as np
        B, S, D_MODEL, D_INNER, D_STATE = (4, 2048, 512, 1024, 16)
        d_inner = W_conv.shape[0]
        d_state = A_log.shape[0]
        xr, gate = jnp.split(x @ W_in.T, 2, axis=-1)
        xr = xr + t_emb[:, None, :]
        xc = jax.lax.conv_general_dilated(xr.transpose(0, 2, 1), W_conv, (1,), [(3, 0)], feature_group_count=d_inner, dimension_numbers=('NCH', 'OIH', 'NCH')) + b_conv[None, :, None]
        xc = jax.nn.silu(xc).transpose(0, 2, 1)
        mu = xc.mean(-1, keepdims=True)
        var = xc.var(-1, keepdims=True)
        xn = (xc - mu) / jnp.sqrt(var + 1e-05) * ln_g + ln_b
        Bm, Cm, dt = jnp.split(xn @ W_xproj.T, 3, axis=-1)
        dt = jnp.tanh(dt @ W_dt.T + b_dt) * 0.01
        A = -jnp.tanh(A_log)
        Ad = 1.0 + dt * A
        Bd = Bm * jnp.minimum(jnp.linalg.norm(xn, axis=-1, keepdims=True), 1.0)
        h0 = jnp.zeros((xn.shape[0], d_state, d_inner), xn.dtype)

        def step(h, inputs):
            ad, bd, xt, ct = inputs
            h = jnp.clip(h * ad[:, :, None] + bd[:, :, None] * xt[:, None, :], -10.0, 10.0)
            yt = jnp.einsum('bd,bdh->bh', ct, h)
            return (h, yt)
        _, ys = jax.lax.scan(step, h0, (Ad.transpose(1, 0, 2), Bd.transpose(1, 0, 2), xn.transpose(1, 0, 2), Cm.transpose(1, 0, 2)))
        y = ys.transpose(1, 0, 2) + D * xn
        return y * jax.nn.silu(gate) @ W_out.T

    def _L1_cond_ref(x, q_weight, k_weight, v_weight, w_weight, u_weight, styles, num_heads):
        import jax, jax.numpy as jnp
        import numpy as np
        EPS_IN = 1e-05
        EPS_DM = 1e-08

        def _dcoef(weight, style):
            return jax.lax.rsqrt(jnp.einsum('oi,bi->bo', jnp.square(weight), jnp.square(style)) + EPS_DM)
        B, S, H = x.shape
        nh = num_heads
        d = H // nh
        scale = jnp.asarray(d, x.dtype) ** (-0.5)
        s1 = styles[:, :H]
        s2 = styles[:, H:]
        x = x * s1[:, None, :]
        mu = jnp.mean(x, axis=-1, keepdims=True)
        var = jnp.mean(jnp.square(x - mu), axis=-1, keepdims=True)
        x = (x - mu) * jax.lax.rsqrt(var + EPS_IN)
        q_dc = _dcoef(q_weight, s1)
        k_dc = _dcoef(k_weight, s1)
        v_dc = _dcoef(v_weight, s1)
        w_dc = _dcoef(w_weight, s2)
        u_dc = _dcoef(u_weight, s2)

        def heads(t):
            return t.reshape(B, S, nh, d).transpose(0, 2, 1, 3)
        q = heads(jnp.einsum('bsh,oh->bso', x, q_weight) * q_dc[:, None, :])
        k = heads(jnp.einsum('bsh,oh->bso', x, k_weight) * k_dc[:, None, :])
        v_flat = jnp.einsum('bsh,oh->bso', x, v_weight) * v_dc[:, None, :] * s2[:, None, :]
        skip = v_flat
        v = heads(v_flat)
        attn = jnp.einsum('bhqd,bhkd->bhqk', q, k) * scale
        attn = jax.nn.softmax(attn, axis=-1)
        out = jnp.einsum('bhqk,bhkd->bhqd', attn, v).transpose(0, 2, 1, 3).reshape(B, S, H)
        out = jnp.einsum('bsh,oh->bso', out, w_weight) * w_dc[:, None, :]
        skip = jnp.einsum('bsh,oh->bso', skip, u_weight) * u_dc[:, None, :]
        return out + skip

    def _L2_cond_ref(x, q_weight, k_weight, v_weight, w_weight, u_weight, styles, num_heads):
        import jax, jax.numpy as jnp
        import numpy as np
        EPS_IN = 1e-05
        EPS_DM = 1e-08

        def _dcoef(weight, style):
            return jax.lax.rsqrt(jnp.einsum('oi,bi->bo', jnp.square(weight), jnp.square(style)) + EPS_DM)
        B, S, H = x.shape
        nh = num_heads
        d = H // nh
        scale = jnp.asarray(d, x.dtype) ** (-0.5)
        s1 = styles[:, :H]
        s2 = styles[:, H:]
        x = x * s1[:, None, :]
        mu = jnp.mean(x, axis=-1, keepdims=True)
        var = jnp.mean(jnp.square(x - mu), axis=-1, keepdims=True)
        x = (x - mu) * jax.lax.rsqrt(var + EPS_IN)
        q_dc = _dcoef(q_weight, s1)
        k_dc = _dcoef(k_weight, s1)
        v_dc = _dcoef(v_weight, s1)
        w_dc = _dcoef(w_weight, s2)
        u_dc = _dcoef(u_weight, s2)

        def heads(t):
            return t.reshape(B, S, nh, d).transpose(0, 2, 1, 3)
        q = heads(jnp.einsum('bsh,oh->bso', x, q_weight) * q_dc[:, None, :])
        k = heads(jnp.einsum('bsh,oh->bso', x, k_weight) * k_dc[:, None, :])
        v_flat = jnp.einsum('bsh,oh->bso', x, v_weight) * v_dc[:, None, :] * s2[:, None, :]
        skip = v_flat
        v = heads(v_flat)
        attn = jnp.einsum('bhqd,bhkd->bhqk', q, k) * scale
        attn = jax.nn.softmax(attn, axis=-1)
        out = jnp.einsum('bhqk,bhkd->bhqd', attn, v).transpose(0, 2, 1, 3).reshape(B, S, H)
        out = jnp.einsum('bsh,oh->bso', out, w_weight) * w_dc[:, None, :]
        skip = jnp.einsum('bsh,oh->bso', skip, u_weight) * u_dc[:, None, :]
        return out + skip

    def _L3_cond_ref(x, t_emb, W_in, W_conv, b_conv, ln_g, ln_b, W_xproj, W_dt, b_dt, A_log, D, W_out):
        import jax, jax.numpy as jnp
        import numpy as np
        B, S, D_MODEL, D_INNER, D_STATE = (4, 2048, 512, 1024, 16)
        d_inner = W_conv.shape[0]
        d_state = A_log.shape[0]
        xr, gate = jnp.split(x @ W_in.T, 2, axis=-1)
        xr = xr + t_emb[:, None, :]
        xc = jax.lax.conv_general_dilated(xr.transpose(0, 2, 1), W_conv, (1,), [(3, 0)], feature_group_count=d_inner, dimension_numbers=('NCH', 'OIH', 'NCH')) + b_conv[None, :, None]
        xc = jax.nn.silu(xc).transpose(0, 2, 1)
        mu = xc.mean(-1, keepdims=True)
        var = xc.var(-1, keepdims=True)
        xn = (xc - mu) / jnp.sqrt(var + 1e-05) * ln_g + ln_b
        Bm, Cm, dt = jnp.split(xn @ W_xproj.T, 3, axis=-1)
        dt = jnp.tanh(dt @ W_dt.T + b_dt) * 0.01
        A = -jnp.tanh(A_log)
        Ad = 1.0 + dt * A
        Bd = Bm * jnp.minimum(jnp.linalg.norm(xn, axis=-1, keepdims=True), 1.0)
        h0 = jnp.zeros((xn.shape[0], d_state, d_inner), xn.dtype)

        def step(h, inputs):
            ad, bd, xt, ct = inputs
            h = jnp.clip(h * ad[:, :, None] + bd[:, :, None] * xt[:, None, :], -10.0, 10.0)
            yt = jnp.einsum('bd,bdh->bh', ct, h)
            return (h, yt)
        _, ys = jax.lax.scan(step, h0, (Ad.transpose(1, 0, 2), Bd.transpose(1, 0, 2), xn.transpose(1, 0, 2), Cm.transpose(1, 0, 2)))
        y = ys.transpose(1, 0, 2) + D * xn
        return y * jax.nn.silu(gate) @ W_out.T
    x = x + _L0_cond_ref(x, cond_2048, L0_cond_W_in, L0_cond_W_conv, L0_cond_b_conv, L0_cond_ln_g, L0_cond_ln_b, L0_cond_W_xproj, L0_cond_W_dt, L0_cond_b_dt, L0_cond_A_log, L0_cond_D, L0_cond_W_out)
    x = x + _L1_cond_ref(x, L1_cond_q_weight, L1_cond_k_weight, L1_cond_v_weight, L1_cond_w_weight, L1_cond_u_weight, cond_2048, 16)
    x = x + _L2_cond_ref(x, L2_cond_q_weight, L2_cond_k_weight, L2_cond_v_weight, L2_cond_w_weight, L2_cond_u_weight, cond_2048, 16)
    x = x + _L3_cond_ref(x, cond_2048, L3_cond_W_in, L3_cond_W_conv, L3_cond_b_conv, L3_cond_ln_g, L3_cond_ln_b, L3_cond_W_xproj, L3_cond_W_dt, L3_cond_b_dt, L3_cond_A_log, L3_cond_D, L3_cond_W_out)
    return x

_drawn_inputs = setup_inputs


def setup_inputs(seed=0):
    import zlib

    import numpy as np

    out = dict(_drawn_inputs(seed))
    spreads = {'L0_cond_b_conv': (0.0, 0.1),
     'L0_cond_ln_g': (1.0, 0.2),
     'L0_cond_ln_b': (0.0, 0.1),
     'L0_cond_D': (0.10000000149011612, 0.6),
     'L3_cond_b_conv': (0.0, 0.1),
     'L3_cond_ln_g': (1.0, 0.2),
     'L3_cond_ln_b': (0.0, 0.1),
     'L3_cond_D': (0.10000000149011612, 0.6)}
    factors = {'L0_cond_W_dt': 22.326,
     'L0_cond_b_dt': 8.0,
     'L0_cond_A_log': 8.0,
     'L3_cond_W_dt': 40.296,
     'L3_cond_b_dt': 8.0,
     'L3_cond_A_log': 8.0}
    for name, (base, spread) in spreads.items():
        noise = np.random.default_rng([zlib.crc32(name.encode()), seed]).standard_normal(out[name].shape)
        drawn = base * np.exp(spread * noise) if base else spread * noise
        out[name] = jnp.asarray(drawn.astype(out[name].dtype))
    for name, factor in factors.items():
        out[name] = (out[name] * factor).astype(out[name].dtype)
    return out
```

```python
import concourse.bass as bass
from concourse import mybir
from contextlib import ExitStack

F32 = mybir.dt.float32
F32R = mybir.dt.float32r
ALU = mybir.AluOpType
ACT = mybir.ActivationFunctionType
AX = mybir.AxisListType

P = 128
B, S, DM = 32, 128, 512
TOK = B * S
DI, NS = 1024, 16
KD, KI = DM // P, DI // P
TB = 4
TW = TB * S
NT = TOK // TW
NPROJ = 3 * NS
LN_EPS = 1e-5
CLIP = 10.0
GJ = 4
GB = B // GJ
TS = 4
NBLK = S // TS


class Phase:

    def __init__(self, nc, tag):
        self.nc, self.tag, self.ctx, self.signals = nc, tag, ExitStack(), []

    def __enter__(self):
        self.ctx.__enter__()
        return self

    def __exit__(self, *a):
        done = self.ctx.__exit__(*a)
        if self.signals:
            self.nc.clear_and_free_semaphores(self.signals)
            self.nc.all_engine_barrier()
        return done

    def sb(self, name, shape, dt=F32):
        return self.ctx.enter_context(self.nc.sbuf_tensor(f"{self.tag}_{name}", shape, dt))

    def ps(self, name, cols=512):
        return self.ctx.enter_context(self.nc.psum_tensor(f"{self.tag}_{name}", [P, cols], F32))

    def sem(self, name):
        signal = self.nc.alloc_semaphore(f"{self.tag}_{name}")
        self.signals.append(signal)
        return signal

    def sems(self, name, n):
        return [self.sem(f"{name}{k}") for k in range(n)]

    def block(self):
        return self.ctx.enter_context(self.nc.Block())


def at_least(eng, sem, value):
    if not (isinstance(value, int) and value <= 0):
        eng.wait_ge(sem, value)


def hold(eng):
    eng.nop(nofuse=True)


def pairs(eng, n, body):
    body(0, True, False)
    with eng.Fori(1, n - 1) as i:
        body(i, False, False)
    body(n - 1, False, True)


def mm3(pe, out, wh, wl, xh, xl, first, last):
    pe.matmul(out, wh, xh, start=first, stop=False)
    pe.matmul(out, wl, xh, start=False, stop=False)
    return pe.matmul(out, wh, xl, start=False, stop=last)


def split_weights(nc, tag, parts):
    with Phase(nc, tag) as ph:
        stage = ph.sb("stage", [P, 2, 2048])
        loaded = ph.sems("loaded", 2)
        high_done, low_done = ph.sem("high"), ph.sem("low")
        block = ph.block()

        @block.sync
        def _(sp):
            for c, (src, hi, lo) in enumerate(parts):
                n = src.shape[1]
                at_least(sp, low_done, c - 1)
                sp.dma_start(stage[:, c % 2, 0:n], src).then_inc(loaded[c % 2], 16)

        @block.scalar
        def _(act):
            for c, (src, hi, lo) in enumerate(parts):
                n = src.shape[1]
                act.wait_ge(loaded[c % 2], 16 * (c // 2 + 1))
                act.activation(hi, stage[:, c % 2, 0:n], ACT.Copy).then_inc(high_done, 1)

        @block.vector
        def _(dve):
            for c, (src, hi, lo) in enumerate(parts):
                n = src.shape[1]
                dve.wait_ge(high_done, c + 1)
                dve.tensor_tensor(lo, stage[:, c % 2, 0:n], hi.bitcast(F32), ALU.subtract).then_inc(low_done, 1)


def scan_layer(nc, tag, x_in, x_out, w, cst, dram):
    with Phase(nc, tag + "s") as keep:
        proj = keep.sb("proj", [P, B, NPROJ])
        stat = keep.sb("stat", [P, B, 4])
        wsum = keep.sb("wsum", [P, NPROJ])
        wbias = keep.sb("wbias", [P, NPROJ])
        project_phase(nc, tag + "a", x_in, w, cst, dram, proj, stat, wsum, wbias)
        with Phase(nc, tag + "k") as keep2:
            coef = keep2.sb("coef", [P, S, 4, GJ])
            coefficient_phase(nc, tag + "b", w, cst, proj, stat, wsum, wbias, coef)
            recurrence_phase(nc, tag + "r", cst, dram, coef)
    output_phase(nc, tag + "o", x_in, x_out, w, cst, dram)


def project_phase(nc, tag, x_in, w, cst, dram, proj, stat, wsum, wbias):
    with Phase(nc, tag) as ph:
        wih = ph.sb("wih", [P, KD, 2 * DI], F32R)
        wil = ph.sb("wil", [P, KD, 2 * DI], F32R)
        w_in = w["W_inT"].rearrange("(k p) n -> p k n", p=P)
        split_weights(nc, tag + "w", [(w_in[:, k, :], wih[:, k, :], wil[:, k, :]) for k in range(KD)])

        temb = ph.sb("temb", [P, KI, B])
        wconv = ph.sb("wconv", [P, KI, 4])
        bconv = ph.sb("bconv", [P, KI])
        gcol = ph.sb("gcol", [P, KI])
        bcol = ph.sb("bcol", [P, KI])
        grow = ph.sb("grow", [P, DI])
        brow = ph.sb("brow", [P, DI])
        drow = ph.sb("drow", [P, DI])
        wxg = ph.sb("wxg", [P, KI, NPROJ])
        ident = ph.sb("ident", [P, P])
        small_weights(nc, tag + "p", w, cst, dict(temb=temb, wconv=wconv, bconv=bconv, gcol=gcol, bcol=bcol,
                      grow=grow, brow=brow, drow=drow, wxg=wxg, ident=ident, wsum=wsum, wbias=wbias))

        xt = ph.sb("xt", [P, KD, TW])
        xh = ph.sb("xh", [P, 2, KD, TW], F32R)
        xl = ph.sb("xl", [P, 2, KD, TW], F32R)
        pad = ph.sb("pad", [P, 2, TB, S + 3])
        acc = ph.sb("acc", [P, 2, TB, S])
        xc = ph.sb("xc", [P, 2, KI, TW])
        gate = ph.sb("gate", [P, 2, TW])
        xn = ph.sb("xn", [P, 2, DI])
        xo = ph.sb("xo", [P, 2, 2, DI], F32R)
        dx = ph.sb("dx", [P, DI])
        junk = ph.sb("junk", [P, DI], mybir.dt.bfloat16)
        raw = ph.sb("raw", [NPROJ, TW])
        bst = ph.sb("bst", [P, 2, 6])
        st = ph.sb("st", [P, 2, TB, 4])
        nmr = ph.sb("nmr", [P, 2])
        veps = ph.sb("veps", [P, 2])
        mhalf = ph.sb("mhalf", [P, 1])
        pxr = [ph.ps(f"pxr{k}") for k in range(2)]
        pg = ph.ps("pg")
        ptr = [ph.ps(f"ptr{k}", 1024) for k in range(2)]
        pp = ph.ps("pp")

        x_loaded, high, low = ph.sem("x_loaded"), ph.sem("high"), ph.sem("low")
        split_used = ph.sem("split_used")
        zeroed, halved = ph.sem("zeroed"), ph.sem("halved")
        xr_mm, g_mm, p_mm, pt_mm, tr_mm = (ph.sem(n) for n in ("xr_mm", "g_mm", "p_mm", "pt_mm", "tr_mm"))
        xr_ev, tap0, taps = (ph.sem(n) for n in ("xr_ev", "tap0", "taps"))
        g_ev, xc_ev, raw_ev, proj_ev = (ph.sem(n) for n in ("g_ev", "xc_ev", "raw_ev", "proj_ev"))
        g_st = ph.sems("g_st", 2)
        bn, var, rstd, nm, z, gz, gb, dxm, xoh, ss, xol, stc = (ph.sem(n) for n in (
            "bn", "var", "rstd", "nm", "z", "gz", "gb", "dxm", "xoh", "ss", "xol", "stc"))
        xo_st, dx_st = ph.sems("xo_st", 2), ph.sem("dx_st")
        block = ph.block()
        x_v = x_in.rearrange("(k p) n -> p k n", p=P)
        gate_v = dram["gate"].rearrange("(k p) n -> p k n", p=P)
        n_pairs = NT // 2

        @block.sync
        def _(sp):
            def load(T):
                at_least(sp, low, T)
                sp.dma_start(xt[:, :, :], x_v[:, :, bass.ds(T * TW, TW)]).then_inc(x_loaded, 16)

            def store_batch(T, b):
                r = b % 2
                n = TB * T + b
                sp.wait_ge(xoh, n + 1)
                sp.wait_ge(xol, n + 1)
                sp.dma_start(dram["xhl"][:, :, bass.ds(n, 1), :].rearrange("t h b i -> t h (b i)"),
                             xo[:, r, :, :].bitcast(F32)).then_inc(xo_st[r], 16)
                sp.wait_ge(dxm, n + 1)
                sp.dma_start(dram["dx"][:, bass.ds(n, 1), :].rearrange("t b i -> t (b i)"),
                             dx[:, :]).then_inc(dx_st, 16)

            def body(i, first, last):
                for q in range(2):
                    T = 2 * i + q
                    if first and q == 0:
                        load(0)
                    for it in range(KI):
                        sp.wait_ge(g_ev, KI * T + it + 1)
                        sp.dma_start(gate_v[:, it, bass.ds(T * TW, TW)], gate[:, it % 2, :]).then_inc(g_st[it % 2], 16)
                        if it == 3 and not (last and q == 1):
                            load(T + 1)
                        if it % 2 == 1 and not (first and q == 0):
                            store_batch(T - 1, it // 2)

            pairs(sp, n_pairs, body)
            for b in range(TB):
                store_batch(NT - 1, b)
            for r in range(2):
                sp.wait_ge(g_st[r], 16 * NT * KI // 2)
                sp.wait_ge(xo_st[r], 16 * B // 2)
            sp.wait_ge(dx_st, 16 * B)

        @block.tensor
        def _(pe):
            def project(T, it, q):
                n = KI * T + it
                if it == 0:
                    pe.wait_ge(low, T + 1)
                at_least(pe, xr_ev, n - 1)
                for k in range(KD):
                    last = mm3(pe, pxr[it % 2][:, :], wih[:, k, it * P:(it + 1) * P], wil[:, k, it * P:(it + 1) * P],
                               xh[:, q, k, :], xl[:, q, k, :], k == 0, k == KD - 1)
                last.then_inc(xr_mm, 1)
                at_least(pe, g_ev, n)
                c = DI + it * P
                for k in range(KD):
                    last = mm3(pe, pg[:, :], wih[:, k, c:c + P], wil[:, k, c:c + P],
                               xh[:, q, k, :], xl[:, q, k, :], k == 0, k == KD - 1)
                last.then_inc(g_mm, 1)

            def xproj(T, q):
                pe.wait_ge(xc_ev, KI * (T + 1))
                at_least(pe, proj_ev, T)
                for k in range(KI):
                    last = pe.matmul(pp[0:NPROJ, :], wxg[:, k, :], xc[:, q, k, :], start=k == 0, stop=k == KI - 1)
                last.then_inc(p_mm, 1)

            def xproj_turn(T):
                pe.wait_ge(raw_ev, T + 1)
                hold(pe)
                for b in range(TB):
                    last = pe.transpose(pp[:, b * NPROJ:(b + 1) * NPROJ], raw[:, b * S:(b + 1) * S],
                                        ident[0:NPROJ, 0:NPROJ])
                last.then_inc(pt_mm, 1)

            def turn(T, b, q):
                n = TB * T + b
                at_least(pe, z, n - 1)
                for k in range(KI):
                    last = pe.transpose(ptr[b % 2][:, k * P:(k + 1) * P], xc[:, q, k, b * S:(b + 1) * S], ident[:, :])
                last.then_inc(tr_mm, 1)

            def body(i, first, last):
                for q in range(2):
                    T = 2 * i + q
                    for it in range(KI):
                        project(T, it, q)
                        if not (first and q == 0):
                            if it == 0:
                                xproj(T - 1, 1 - q)
                            if it == 1:
                                xproj_turn(T - 1)
                            if it % 2 == 1:
                                turn(T - 1, it // 2, 1 - q)

            pairs(pe, n_pairs, body)
            xproj(NT - 1, 1)
            xproj_turn(NT - 1)
            for b in range(TB):
                turn(NT - 1, b, 1)

        @block.scalar
        def _(act):
            def split_high(T, q):
                act.wait_ge(x_loaded, 16 * (T + 1))
                at_least(act, g_mm, KI * (T - 1))
                act.activation(xh[:, q, :, :], xt[:, :, :], ACT.Copy).then_inc(high, 1)

            def silu_conv(T, it, q):
                n = KI * T + it
                act.wait_ge(taps, 3 * (n + 1))
                if it == 0:
                    at_least(act, tr_mm, TB * (T - 1))
                act.activation(xc[:, q, it, :], acc[:, it % 2, :, :].rearrange("p b s -> p (b s)"), ACT.Silu)\
                   .then_inc(xc_ev, 1)

            def main(T, it, q):
                n = KI * T + it
                act.wait_ge(xr_ev, n + 1)
                at_least(act, xc_ev, n - 1)
                act.activation(acc[:, it % 2, :, :], pad[:, it % 2, :, 3:3 + S], ACT.Identity,
                               bias=bconv[:, it:it + 1], scale=wconv[:, it, 3:4]).then_inc(tap0, 1)
                act.wait_ge(g_mm, n + 1)
                at_least(act, g_st[it % 2], 16 * (KI // 2 * T + it // 2))
                act.activation(gate[:, it % 2, :], pg[:, :], ACT.Silu).then_inc(g_ev, 1)
                if it:
                    silu_conv(T, it - 1, q)

            def copy_raw(T):
                act.wait_ge(p_mm, T + 1)
                act.activation(raw[:, :], pp[0:NPROJ, :], ACT.Copy).then_inc(raw_ev, 1)

            def normalise(T, b, q):
                r, n = b % 2, TB * T + b
                act.wait_ge(nm, n + 1)
                at_least(act, dxm, n - 1)
                at_least(act, ss, n - 1)
                at_least(act, xol, n - 1)
                act.activation(xn[:, r, :], ptr[r][:, :], ACT.Identity, bias=nmr[:, r:r + 1],
                               scale=st[:, q, b, 2:3]).then_inc(z, 1)

            def halves(T, b, q):
                r, n = b % 2, TB * T + b
                act.wait_ge(gb, n + 1)
                at_least(act, xo_st[r], 16 * (TB // 2 * T + b // 2))
                act.activation(xo[:, r, 0, :], xn[:, r, :], ACT.Copy).then_inc(xoh, 1)
                act.activation(junk[:, :], xn[:, r, :], ACT.Square, accum_out=st[:, q, b, 3:4]).then_inc(ss, 1)

            def body(i, first, last):
                for q in range(2):
                    T = 2 * i + q
                    if first and q == 0:
                        split_high(0, 0)
                    for it in range(KI):
                        main(T, it, q)
                        tail = not (first and q == 0)
                        if tail and it == 0:
                            copy_raw(T - 1)
                        if tail and it % 2 == 0 and it:
                            halves(T - 1, it // 2 - 1, 1 - q)
                        if tail and it % 2 == 1:
                            normalise(T - 1, it // 2, 1 - q)
                        if it == 4 and not (last and q == 1):
                            split_high(T + 1, 1 - q)
                    silu_conv(T, KI - 1, q)
                    if not (first and q == 0):
                        halves(T - 1, TB - 1, 1 - q)

            pairs(act, n_pairs, body)
            copy_raw(NT - 1)
            for b in range(TB):
                normalise(NT - 1, b, 1)
                halves(NT - 1, b, 1)

        @block.vector
        def _(dve):
            def split_low(T, q):
                dve.wait_ge(high, T + 1)
                dve.tensor_tensor(xl[:, q, :, :], xt[:, :, :], xh[:, q, :, :].bitcast(F32), ALU.subtract)\
                   .then_inc(low, 1)

            def evacuate(T, it):
                n = KI * T + it
                dve.wait_ge(xr_mm, n + 1)
                at_least(dve, taps, 3 * (n - 1))
                at_least(dve, tap0, n - 1)
                t = temb[:, it, bass.ds(T * TB, TB)].unsqueeze(2).to_broadcast([P, TB, S])
                dve.tensor_tensor(pad[:, it % 2, :, 3:3 + S], pxr[it % 2][:, :].rearrange("p (b s) -> p b s", b=TB),
                                  t, ALU.add).then_inc(xr_ev, 1)

            def add_taps(T, it):
                n = KI * T + it
                dve.wait_ge(tap0, n + 1)
                dve.wait_ge(xr_ev, n + 1)
                for c in range(3):
                    a = acc[:, it % 2, :, :]
                    if c:
                        dve.wait_ge(taps, 3 * n + c)
                    done = dve.scalar_tensor_tensor(out=a, in0=pad[:, it % 2, :, c:c + S], scalar=wconv[:, it, c:c + 1],
                                                    in1=a, op0=ALU.mult, op1=ALU.add)
                    done.then_inc(taps, 1)

            def statistics(T, b, q):
                n = TB * T + b
                dve.wait_ge(tr_mm, n + 1)
                at_least(dve, bn, 3 * n)
                dve.bn_stats(bst[:, 0, :], ptr[b % 2][:, 0:512]).then_inc(bn, 1)
                dve.bn_stats(bst[:, 1, :], ptr[b % 2][:, 512:1024]).then_inc(bn, 1)
                dve.wait_ge(bn, 3 * n + 2)
                if b == 0:
                    at_least(dve, stc, T - 1)
                hold(dve)
                dve.bn_aggr(st[:, q, b, 0:2], bst[:, :, :].rearrange("p a c -> p (a c)")).then_inc(bn, 1)
                dve.wait_ge(bn, 3 * n + 3)
                at_least(dve, rstd, n - 1)
                dve.tensor_scalar(veps[:, b % 2:b % 2 + 1], st[:, q, b, 1:2], LN_EPS, None, ALU.add).then_inc(var, 1)

            def low_half(T, b):
                r, n = b % 2, TB * T + b
                dve.wait_ge(xoh, n + 1)
                dve.tensor_tensor(xo[:, r, 1, :], xn[:, r, :], xo[:, r, 0, :].bitcast(F32), ALU.subtract)\
                   .then_inc(xol, 1)

            def keep_projection(T):
                dve.wait_ge(pt_mm, T + 1)
                dve.tensor_copy(proj[:, bass.ds(T * TB, TB), :],
                                pp[:, 0:TB * NPROJ].rearrange("p (b c) -> p b c", b=TB)).then_inc(proj_ev, 1)

            def keep_statistics(T, q):
                dve.wait_ge(ss, TB * (T + 1))
                dve.tensor_copy(stat[:, bass.ds(T * TB, TB), :], st[:, q, :, :]).then_inc(stc, 1)

            dve.memset(pad[:, :, :, 0:3], 0.0).then_inc(zeroed, 1)
            dve.memset(mhalf[:, :], -0.5).then_inc(halved, 1)
            dve.wait_ge(zeroed, 1)

            def body(i, first, last):
                for q in range(2):
                    T = 2 * i + q
                    if first and q == 0:
                        split_low(0, 0)
                    evacuate(T, 0)
                    for it in range(KI):
                        if it + 1 < KI:
                            evacuate(T, it + 1)
                        add_taps(T, it)
                        tail = not (first and q == 0)
                        if tail and it == 1:
                            keep_projection(T - 1)
                        if tail and it % 2 == 0 and it:
                            low_half(T - 1, it // 2 - 1)
                        if tail and it % 2 == 1:
                            statistics(T - 1, it // 2, 1 - q)
                        if it == 4 and not (last and q == 1):
                            split_low(T + 1, 1 - q)
                    if not (first and q == 0):
                        low_half(T - 1, TB - 1)
                        keep_statistics(T - 1, 1 - q)

            pairs(dve, n_pairs, body)
            keep_projection(NT - 1)
            for b in range(TB):
                statistics(NT - 1, b, 1)
                low_half(NT - 1, b)
            keep_statistics(NT - 1, 1)

        @block.gpsimd
        def _(pool):
            pool.wait_ge(halved, 1)

            def batch(T, b, q):
                r, n = b % 2, TB * T + b
                pool.wait_ge(var, n + 1)
                pool.tensor_tensor(st[:, q, b, 2:3], veps[:, r:r + 1], mhalf[:, :], ALU.pow).then_inc(rstd, 1)
                pool.wait_ge(rstd, n + 1)
                at_least(pool, z, n - 1)
                hold(pool)
                pool.tensor_scalar(nmr[:, r:r + 1], st[:, q, b, 0:1], st[:, q, b, 2:3], -1.0, ALU.mult, ALU.mult)\
                    .then_inc(nm, 1)
                pool.wait_ge(z, n + 1)
                pool.tensor_tensor(xn[:, r, :], xn[:, r, :], grow[:, :], ALU.mult).then_inc(gz, 1)
                pool.wait_ge(gz, n + 1)
                pool.tensor_tensor(xn[:, r, :], xn[:, r, :], brow[:, :], ALU.add).then_inc(gb, 1)
                pool.wait_ge(gb, n + 1)
                at_least(pool, dx_st, 16 * n)
                pool.tensor_tensor(dx[:, :], xn[:, r, :], drow[:, :], ALU.mult).then_inc(dxm, 1)

            def body(i, first, last):
                for q in range(2):
                    if not (first and q == 0):
                        for b in range(TB):
                            batch(2 * i + q - 1, b, 1 - q)

            pairs(pool, n_pairs, body)
            for b in range(TB):
                batch(NT - 1, b, 1)


def small_weights(nc, tag, w, cst, t):
    with Phase(nc, tag) as ph:
        wx = ph.sb("wx", [P, KI, NPROJ])
        wxb = ph.sb("wxb", [P, KI, NPROJ])
        wxdt = ph.sb("wxdt", [NS, DI])
        wdt = ph.sb("wdt", [NS, NS])
        bdt = ph.sb("bdt", [P, NS])
        ones = ph.sb("ones", [P, P])
        pf, psum_s, psum_b = ph.ps("pf"), ph.ps("ps"), ph.ps("pb")
        loaded, folded, copied, scaled, summed, kept = (ph.sem(n) for n in (
            "loaded", "folded", "copied", "scaled", "summed", "kept"))
        block = ph.block()
        loads = [(t["temb"][:, :, :], w["tembT"].rearrange("(k p) b -> p k b", p=P)),
                 (t["wconv"][:, :, :], w["W_conv"].rearrange("(k p) a c -> p k (a c)", p=P)),
                 (t["bconv"][:, :], w["b_convT"]),
                 (t["gcol"][:, :], w["ln_gT"]), (t["bcol"][:, :], w["ln_bT"]),
                 (t["grow"][:, :], w["ln_g"].partition_broadcast(P)),
                 (t["brow"][:, :], w["ln_b"].partition_broadcast(P)),
                 (t["drow"][:, :], w["D"].partition_broadcast(P)),
                 (t["ident"][:, :], cst["ident"]),
                 (wx[:, :, :], w["W_xprojT"].rearrange("(k p) c -> p k c", p=P)),
                 (wxdt[:, :], w["W_xproj"][2 * NS:NPROJ, :]),
                 (wdt[:, :], w["W_dtT"]),
                 (bdt[:, :], w["b_dt"].partition_broadcast(P))]

        @block.sync
        def _(sp):
            for dst, src in loads:
                sp.dma_start(dst, src).then_inc(loaded, 16)
            sp.wait_ge(loaded, 16 * len(loads))

        @block.tensor
        def _(pe):
            pe.wait_ge(loaded, 16 * len(loads))
            for k in range(KI):
                last = pe.matmul(pf[:, k * NS:(k + 1) * NS], wxdt[:, k * P:(k + 1) * P], wdt[:, :], start=True, stop=True)
            last.then_inc(folded, 1)
            pe.wait_ge(scaled, 3)
            for k in range(KI):
                pe.matmul(psum_s[:, 0:NPROJ], ones[:, :], t["wxg"][:, k, :], start=k == 0, stop=k == KI - 1)
            for k in range(KI):
                last = pe.matmul(psum_b[:, 0:NPROJ], ones[:, :], wxb[:, k, :], start=k == 0, stop=k == KI - 1)
            last.then_inc(summed, 1)

        @block.vector
        def _(dve):
            dve.memset(ones[:, :], 1.0).then_inc(scaled, 1)
            dve.wait_ge(loaded, 16 * len(loads))
            dve.wait_ge(folded, 1)
            dve.tensor_copy(wx[:, :, 2 * NS:NPROJ], pf[:, 0:KI * NS].rearrange("p (k c) -> p k c", k=KI))\
               .then_inc(copied, 1)
            dve.wait_ge(copied, 1)
            for dst, col in ((t["wxg"], t["gcol"]), (wxb, t["bcol"])):
                dve.tensor_tensor(dst[:, :, :], wx[:, :, :], col[:, :].unsqueeze(2).to_broadcast([P, KI, NPROJ]),
                                  ALU.mult).then_inc(scaled, 1)
            dve.wait_ge(summed, 1)
            dve.tensor_copy(t["wsum"][:, :], psum_s[:, 0:NPROJ]).then_inc(kept, 1)
            dve.tensor_copy(t["wbias"][:, 0:2 * NS], psum_b[:, 0:2 * NS]).then_inc(kept, 1)
            dve.tensor_tensor(t["wbias"][:, 2 * NS:NPROJ], psum_b[:, 2 * NS:NPROJ], bdt[:, :], ALU.add).then_inc(kept, 1)
            dve.wait_ge(kept, 3)


def coefficient_phase(nc, tag, w, cst, proj, stat, wsum, wbias, coef):
    with Phase(nc, tag) as ph:
        ident = ph.sb("ident", [P, P])
        alog = ph.sb("alog", [P, 1])
        acol = ph.sb("acol", [P, 2])
        half = ph.sb("half", [P, 1])
        mean_w = ph.sb("mean_w", [P, B, NPROJ])
        norm = ph.sb("norm", [P, B])
        parts = [ph.sb(f"part{c}", [P, B, NS]) for c in range(3)]
        decay = ph.sb("decay", [P, GJ, S])
        zero = ph.sb("zero", [P, S])
        prod = ph.sb("prod", [P, GJ, S])
        inv = ph.sb("inv", [P, GJ, S])
        pt = [ph.ps(f"pt{c}") for c in range(3)]
        loaded, root, step, turned, tanh = (ph.sem(n) for n in ("loaded", "root", "step", "turned", "tanh"))
        block = ph.block()

        @block.sync
        def _(sp):
            sp.dma_start(ident[:, :], cst["ident"]).then_inc(loaded, 16)
            for b in range(GB):
                sp.dma_start(alog[b * NS:(b + 1) * NS, :], w["A_log"].rearrange("(n a) -> n a", a=1)).then_inc(loaded, 16)

        @block.gpsimd
        def _(pool):
            pool.memset(half[:, :], 0.5).then_inc(root, 1)
            pool.wait_ge(root, 1)
            pool.tensor_tensor(norm[:, :], stat[:, :, 3], half[:, :].to_broadcast([P, B]), ALU.pow).then_inc(root, 1)

        @block.vector
        def _(dve):
            count = [0]

            def chain(ins):
                count[0] += 1
                ins.then_inc(step, 1)
                dve.wait_ge(step, count[0])

            full = [P, B, NPROJ]
            chain(dve.tensor_tensor(mean_w[:, :, :], stat[:, :, 0].unsqueeze(2).to_broadcast(full),
                                    wsum[:, :].unsqueeze(1).to_broadcast(full), ALU.mult))
            chain(dve.tensor_tensor(proj[:, :, :], proj[:, :, :], mean_w[:, :, :], ALU.subtract))
            chain(dve.tensor_tensor(proj[:, :, :], proj[:, :, :], stat[:, :, 2].unsqueeze(2).to_broadcast(full), ALU.mult))
            chain(dve.tensor_tensor(proj[:, :, :], proj[:, :, :], wbias[:, :].unsqueeze(1).to_broadcast(full), ALU.add))
            dve.wait_ge(root, 2)
            chain(dve.tensor_scalar(norm[:, :], norm[:, :], 1.0, None, ALU.min))
            chain(dve.tensor_tensor(parts[0][:, :, :], proj[:, :, 0:NS], norm[:, :].unsqueeze(2).to_broadcast([P, B, NS]),
                                    ALU.mult))
            chain(dve.tensor_copy(parts[1][:, :, :], proj[:, :, NS:2 * NS]))
            chain(dve.tensor_copy(parts[2][:, :, :], proj[:, :, 2 * NS:NPROJ]))
            chain(dve.memset(zero[:, :], 0.0))
            dve.wait_ge(tanh, 2)
            chain(dve.tensor_scalar(acol[:, 1:2], acol[:, 0:1], -0.01, None, ALU.mult))
            chain(dve.tensor_scalar(decay[:, :, :], decay[:, :, :], acol[:, 1:2], 1.0, ALU.mult, ALU.add))
            for j in range(GJ):
                chain(dve.tensor_tensor_scan(prod[:, j, :], decay[:, j, :], zero[:, :], 1.0, ALU.mult, ALU.add))
            chain(dve.reciprocal(inv[:, :, :], prod[:, :, :]))
            out = [coef[:, :, c, :].rearrange("p s j -> p j s") for c in range(4)]
            chain(dve.tensor_scalar(out[0], inv[:, :, :], CLIP, None, ALU.mult))
            chain(dve.tensor_scalar(out[1], inv[:, :, :], -CLIP, None, ALU.mult))
            turn = [pt[c][:, :].rearrange("p (j s) -> p j s", j=GJ) for c in range(2)]
            dve.wait_ge(turned, 1)
            chain(dve.tensor_tensor(out[2], turn[0], inv[:, :, :], ALU.mult))
            chain(dve.tensor_tensor(out[3], turn[1], prod[:, :, :], ALU.mult))

        @block.tensor
        def _(pe):
            pe.wait_ge(loaded, 16 * (1 + GB))
            pe.wait_ge(step, 8)
            for c in range(3):
                for j in range(GJ):
                    last = pe.transpose(pt[c][:, j * S:(j + 1) * S],
                                        parts[c][:, j * GB:(j + 1) * GB, :].rearrange("p b n -> p (b n)"), ident[:, :])
            last.then_inc(turned, 1)

        @block.scalar
        def _(act):
            act.wait_ge(loaded, 16 * (1 + GB))
            act.activation(acol[:, 0:1], alog[:, :], ACT.Tanh).then_inc(tanh, 1)
            act.wait_ge(turned, 1)
            act.activation(decay[:, :, :].rearrange("p j s -> p (j s)"), pt[2][:, :], ACT.Tanh).then_inc(tanh, 1)


def recurrence_phase(nc, tag, cst, dram, coef):
    HALF = DI // 2
    with Phase(nc, tag) as ph:
        pick = ph.sb("pick", [2 * B, GJ, P], F32R)
        pickf = ph.sb("pickf", [2 * B, GJ, P])
        ymask = ph.sb("ymask", [P, TS, TS * GB])
        x = ph.sb("x", [2 * B, 2, TS, DI], F32R)
        cf = ph.sb("cf", [P, 2, TS, 4, GJ])
        cd = ph.sb("cd", [P, 2, TS, GJ, TS * GB])
        v = ph.sb("v", [P, GJ, DI])
        g = ph.sb("g", [P, 2, GJ, DI])
        dxt = ph.sb("dxt", [P, 2, DI])
        y = ph.sb("y", [P, 2, DI])
        pv = [ph.ps(f"pv{k}", DI) for k in range(2)]
        py = [ph.ps(f"py{k}", DI) for k in range(2)]
        const, picked = ph.sem("const"), ph.sem("picked")
        x_ld, dx_ld, y_st = ph.sems("x_ld", 2), ph.sems("dx_ld", 2), ph.sems("y_st", 2)
        cfc, cdm, bmm, vev, gup, ymm, yad = (ph.sem(n) for n in ("cfc", "cdm", "bmm", "vev", "gup", "ymm", "yad"))
        block = ph.block()
        n_pairs = NBLK // 2

        @block.sync
        def _(sp):
            sp.dma_start(pickf[:, :, :], cst["pick"]).then_inc(const, 16)
            sp.dma_start(ymask[:, :, :], cst["ymask"]).then_inc(const, 16)

            def load(k, q):
                at_least(sp, bmm, GJ * TS * (k - 1))
                sp.dma_start(x[:, q, :, :].bitcast(F32), dram["xhl"][bass.ds(k * TS, TS), :, :, :].rearrange("t h b i -> (h b) t i"))\
                    .then_inc(x_ld[q], 16)
                at_least(sp, yad, k - 1)
                for j in range(GJ):
                    sp.dma_start(dxt[j * TS * GB:(j + 1) * TS * GB, q, :],
                                 dram["dx"][bass.ds(k * TS, TS), j * GB:(j + 1) * GB, :])\
                        .then_inc(dx_ld[q], 16)

            def store(k, q):
                sp.wait_ge(yad, k + 1)
                for j in range(GJ):
                    sp.dma_start(dram["y"][bass.ds(k * TS, TS), j * GB:(j + 1) * GB, :],
                                 y[j * TS * GB:(j + 1) * TS * GB, q, :]).then_inc(y_st[q], 16)

            def body(i, first, last):
                for q in range(2):
                    k = 2 * i + q
                    if first and q == 0:
                        load(0, 0)
                    if not (last and q == 1):
                        load(k + 1, 1 - q)
                    if not (first and q == 0):
                        store(k - 1, 1 - q)

            pairs(sp, n_pairs, body)
            store(NBLK - 1, 1)
            for q in range(2):
                sp.wait_ge(y_st[q], 16 * GJ * n_pairs)

        @block.gpsimd
        def _(pool):
            pool.wait_ge(const, 32)

            def body(i, first, last):
                for q in range(2):
                    k = 2 * i + q
                    at_least(pool, gup, GJ * (TS * (k - 1) + 1))
                    at_least(pool, vev, GJ * TS * (k - 1))
                    pool.tensor_copy(cf[:, q, :, :, :].rearrange("p t c j -> p (t c j)"),
                                     coef[:, bass.ds(k * TS, TS), :, :].rearrange("p t c j -> p (t c j)"))\
                        .then_inc(cfc, 1)
                    pool.wait_ge(cfc, k + 1)
                    at_least(pool, ymm, TS * (k - 1))
                    for t in range(TS):
                        shape = [P, GJ, TS * GB]
                        last_op = pool.tensor_tensor(cd[:, q, t, :, :], ymask[:, t, :].unsqueeze(1).to_broadcast(shape),
                                                     cf[:, q, t, 3, :].unsqueeze(2).to_broadcast(shape), ALU.mult)
                        last_op.then_inc(cdm, 1)

            pairs(pool, n_pairs, body)

        @block.tensor
        def _(pe):
            pe.wait_ge(picked, 1)

            def spread(s, t, q, j):
                n = GJ * s + j
                at_least(pe, vev, n - 1)
                for h in range(2):
                    last = pe.matmul(pv[j % 2][:, h * HALF:(h + 1) * HALF], pick[:, j, :],
                                     x[:, q, t, h * HALF:(h + 1) * HALF], start=True, stop=True)
                last.then_inc(bmm, 1)

            def read_out(s, k, t, q):
                pe.wait_ge(gup, GJ * (s + 2))
                pe.wait_ge(cdm, TS * k + t + 1)
                if t == 0:
                    at_least(pe, yad, k - 1)
                for h in range(2):
                    for j in range(GJ):
                        last = pe.matmul(py[q][j * TS * GB:(j + 1) * TS * GB, h * HALF:(h + 1) * HALF], cd[:, q, t, j, :],
                                         g[:, t % 2, j, h * HALF:(h + 1) * HALF], start=t == 0, stop=t == TS - 1)
                last.then_inc(ymm, 1)

            def body(i, first, last):
                for q in range(2):
                    k = 2 * i + q
                    pe.wait_ge(x_ld[q], 16 * (i + 1))
                    for t in range(TS):
                        s = TS * k + t
                        spread(s, t, q, 0)
                        spread(s, t, q, 1)
                        if t:
                            read_out(s - 1, k, t - 1, q)
                        elif not (first and q == 0):
                            read_out(s - 1, k - 1, TS - 1, 1 - q)
                        spread(s, t, q, 2)
                        spread(s, t, q, 3)

            pairs(pe, n_pairs, body)
            read_out(S - 1, NBLK - 1, TS - 1, 1)

        @block.scalar
        def _(act):
            act.wait_ge(const, 32)
            act.activation(pick[:, :, :], pickf[:, :, :], ACT.Copy).then_inc(picked, 1)

            def body(i, first, last):
                for q in range(2):
                    k = 2 * i + q
                    act.wait_ge(cfc, k + 1)
                    for t in range(TS):
                        for j in range(GJ):
                            n = GJ * (TS * k + t) + j
                            act.wait_ge(bmm, n + 1)
                            at_least(act, gup, n + 1)
                            act.activation(v[:, j, :], pv[j % 2][:, :], ACT.Copy, scale=cf[:, q, t, 2, j:j + 1])\
                               .then_inc(vev, 1)

            pairs(act, n_pairs, body)

        @block.vector
        def _(dve):
            dve.memset(g[:, 1, :, :], 0.0).then_inc(gup, GJ)

            def add_dx(k, q, uses):
                dve.wait_ge(ymm, TS * (k + 1))
                dve.wait_ge(dx_ld[q], 16 * GJ * uses)
                at_least(dve, y_st[q], 16 * GJ * (uses - 1))
                dve.tensor_tensor(y[:, q, :], py[q][:, :], dxt[:, q, :], ALU.add).then_inc(yad, 1)

            def body(i, first, last):
                for q in range(2):
                    k = 2 * i + q
                    dve.wait_ge(cfc, k + 1)
                    for t in range(TS):
                        s = TS * k + t
                        for j in range(GJ):
                            n = GJ * s + j
                            if j == 0:
                                at_least(dve, ymm, s - 1)
                            dve.wait_ge(gup, n + 1)
                            dve.wait_ge(vev, n + 1)
                            hold(dve)
                            dve._custom_dve(bass.dve_ops.TENSOR_ADD_SAT, out=g[:, t % 2, j, :],
                                            in0=g[:, 1 - t % 2, j, :], in1=v[:, j, :],
                                            s0=cf[:, q, t, 0, j:j + 1], s1=cf[:, q, t, 1, j:j + 1]).then_inc(gup, 1)
                        if t == 1 and not (first and q == 0):
                            add_dx(k - 1, 1 - q, i + q)

            pairs(dve, n_pairs, body)
            add_dx(NBLK - 1, 1, n_pairs)


def output_phase(nc, tag, x_in, x_out, w, cst, dram):
    with Phase(nc, tag) as ph:
        woh = ph.sb("woh", [P, KI, DM], F32R)
        wol = ph.sb("wol", [P, KI, DM], F32R)
        w_out = w["W_outT"].rearrange("(k p) n -> p k n", p=P)
        split_weights(nc, tag + "w", [(w_out[:, k, :], woh[:, k, :], wol[:, k, :]) for k in range(KI)])
        ident = ph.sb("ident", [P, P])
        yt = ph.sb("yt", [P, 2, TB, DI])
        gt = ph.sb("gt", [P, 2, KI, TW])
        xt = ph.sb("xt", [P, 2, KD, TW])
        zt = ph.sb("zt", [P, 2, TW])
        zh = ph.sb("zh", [P, 2, TW], F32R)
        zl = ph.sb("zl", [P, 2, TW], F32R)
        ptr = [ph.ps(f"ptr{k}") for k in range(4)]
        pout = [ph.ps(f"pout{k}") for k in range(KD)]
        const = ph.sem("const")
        y_ld, g_ld, x_ld, x_st = (ph.sems(n, 2) for n in ("y_ld", "g_ld", "x_ld", "x_st"))
        trm, gated, high, low, omm, res = (ph.sem(n) for n in ("trm", "gated", "high", "low", "omm", "res"))
        block = ph.block()
        x_v = x_in.rearrange("(k p) n -> p k n", p=P)
        o_v = x_out.rearrange("(k p) n -> p k n", p=P)
        gate_v = dram["gate"].rearrange("(k p) n -> p k n", p=P)
        n_pairs = NT // 2
        LEAD = 2

        @block.sync
        def _(sp):
            sp.dma_start(ident[:, :], cst["ident"]).then_inc(const, 16)

            def load(T, q):
                at_least(sp, trm, KI * (T - 1))
                sp.dma_start(yt[:, q, :, :], dram["y"][:, bass.ds(T * TB, TB), :]).then_inc(y_ld[q], 16)
                at_least(sp, gated, KI * (T - 1))
                sp.dma_start(gt[:, q, :, :], gate_v[:, :, bass.ds(T * TW, TW)]).then_inc(g_ld[q], 16)

            def load_x(T, q, i):
                at_least(sp, x_st[q], 16 * i)
                sp.dma_start(xt[:, q, :, :], x_v[:, :, bass.ds(T * TW, TW)]).then_inc(x_ld[q], 16)

            def store(T, q):
                sp.wait_ge(res, KD * (T + 1))
                sp.dma_start(o_v[:, :, bass.ds(T * TW, TW)], xt[:, q, :, :]).then_inc(x_st[q], 16)

            def body(i, first, last):
                for q in range(2):
                    T = 2 * i + q
                    if first and q == 0:
                        load(0, 0)
                        load_x(0, 0, 0)
                    if not (last and q == 1):
                        load(T + 1, 1 - q)
                    if not (first and q == 0):
                        store(T - 1, 1 - q)
                    if not (last and q == 1):
                        load_x(T + 1, 1 - q, i + q)

            pairs(sp, n_pairs, body)
            store(NT - 1, 1)
            for q in range(2):
                sp.wait_ge(x_st[q], 16 * n_pairs)

        @block.tensor
        def _(pe):
            pe.wait_ge(const, 16)

            def turn(T, k, q, i):
                n = KI * T + k
                if k == 0:
                    pe.wait_ge(y_ld[q], 16 * (i + 1))
                at_least(pe, gated, n - 3)
                for b in range(TB):
                    last = pe.transpose(ptr[k % 4][:, b * S:(b + 1) * S], yt[:, q, b, k * P:(k + 1) * P], ident[:, :])
                last.then_inc(trm, 1)

            def project(T, k, q):
                n = KI * T + k
                pe.wait_ge(low, n + 1)
                if k == 0:
                    at_least(pe, res, KD * T)
                for m in range(KD):
                    last = mm3(pe, pout[m][:, :], woh[:, k, m * P:(m + 1) * P], wol[:, k, m * P:(m + 1) * P],
                               zh[:, k % 2, :], zl[:, k % 2, :], k == 0, k == KI - 1)
                last.then_inc(omm, 1)

            def body(i, first, last):
                for q in range(2):
                    T = 2 * i + q
                    if first and q == 0:
                        for k in range(LEAD):
                            turn(0, k, 0, 0)
                    for k in range(KI):
                        if k + LEAD < KI:
                            turn(T, k + LEAD, q, i)
                        elif not (last and q == 1):
                            turn(T + 1, k + LEAD - KI, 1 - q, i + q)
                        project(T, k, q)

            pairs(pe, n_pairs, body)

        @block.vector
        def _(dve):
            def gating(T, k, q, i):
                n = KI * T + k
                if k == 0:
                    dve.wait_ge(g_ld[q], 16 * (i + 1))
                dve.wait_ge(trm, n + 1)
                at_least(dve, high, n - 1)
                at_least(dve, low, n - 1)
                dve.tensor_tensor(zt[:, k % 2, :], ptr[k % 4][:, :], gt[:, q, k, :], ALU.mult).then_inc(gated, 1)

            def residual(T, q, i):
                dve.wait_ge(omm, KI * (T + 1))
                dve.wait_ge(x_ld[q], 16 * (i + 1))
                for m in range(KD):
                    dve.tensor_tensor(xt[:, q, m, :], xt[:, q, m, :], pout[m][:, :], ALU.add).then_inc(res, 1)

            def body(i, first, last):
                for q in range(2):
                    T = 2 * i + q
                    for k in range(KI):
                        gating(T, k, q, i)
                        if k == 0 and not (first and q == 0):
                            residual(T - 1, 1 - q, i + q - 1)

            pairs(dve, n_pairs, body)
            residual(NT - 1, 1, n_pairs - 1)

        @block.scalar
        def _(act):
            def body(i, first, last):
                for q in range(2):
                    T = 2 * i + q
                    for k in range(KI):
                        n = KI * T + k
                        act.wait_ge(gated, n + 1)
                        at_least(act, omm, n - 1)
                        act.activation(zh[:, k % 2, :], zt[:, k % 2, :], ACT.Copy).then_inc(high, 1)

            pairs(act, n_pairs, body)

        @block.gpsimd
        def _(pool):
            def body(i, first, last):
                for q in range(2):
                    T = 2 * i + q
                    for k in range(KI):
                        n = KI * T + k
                        pool.wait_ge(high, n + 1)
                        pool.tensor_tensor(zl[:, k % 2, :], zt[:, k % 2, :],
                                           zh[:, k % 2, :].bitcast(F32), ALU.subtract).then_inc(low, 1)

            pairs(pool, n_pairs, body)


NHEAD = 16
DH = DM // NHEAD
HG = 4
NG = NHEAD // HG
UNITS = NG * TB
DEMOD_EPS = 1e-8


def attention_layer(nc, tag, x_in, x_out, w, cst, dram):
    with Phase(nc, tag + "c") as keep:
        dc = keep.sb("dc", [P, 5, KD, B])
        s1 = keep.sb("s1", [P, KD, B])
        demodulation_phase(nc, tag + "d", w, dc, s1)
        heads_phase(nc, tag + "h", x_in, w, cst, dram, dc, s1)
        mix_phase(nc, tag + "m", x_in, x_out, w, cst, dram, dc)


def demodulation_phase(nc, tag, w, dc, s1):
    with Phase(nc, tag) as ph:
        wt = ph.sb("wt", [P, 2, KD, DM])
        sq = ph.sb("sq", [P, 2, KD, DM])
        cond = ph.sb("cond", [P, 2 * KD, B])
        cond2 = ph.sb("cond2", [P, 2 * KD, B])
        ident = ph.sb("ident", [B, B])
        rows = ph.sb("rows", [B, 2, DM])
        val = ph.sb("val", [P, 5, KD, B])
        root = ph.sb("root", [P, 5, KD, B])
        tmp = ph.sb("tmp", [P, 5, KD, B])
        pd = [ph.ps(f"pd{k}") for k in range(2)]
        pt = [ph.ps(f"pt{k}") for k in range(2)]
        loaded, const = ph.sems("loaded", 2), ph.sem("const")
        styled, squared, summed, copied, turned, kept, rooted, step = (ph.sem(n) for n in (
            "styled", "squared", "summed", "copied", "turned", "kept", "rooted", "step"))
        block = ph.block()

        @block.sync
        def _(sp):
            sp.dma_start(cond[:, :, :], w["condT"].rearrange("(k p) b -> p k b", p=P)).then_inc(const, 16)
            sp.dma_start(ident[:, :], w["ident"][0:B, 0:B]).then_inc(const, 16)
            for c, name in enumerate("qkvwu"):
                at_least(sp, squared, c - 1)
                sp.dma_start(wt[:, c % 2, :, :], w[name + "T"].rearrange("(k p) n -> p k n", p=P))\
                    .then_inc(loaded[c % 2], 16)

        @block.scalar
        def _(act):
            act.wait_ge(const, 32)
            act.activation(cond2[:, :, :], cond[:, :, :], ACT.Square).then_inc(styled, 1)
            for c in range(5):
                act.wait_ge(loaded[c % 2], 16 * (c // 2 + 1))
                at_least(act, summed, c - 1)
                act.activation(sq[:, c % 2, :, :], wt[:, c % 2, :, :], ACT.Square).then_inc(squared, 1)
            act.wait_ge(kept, 6)
            act.activation(root[:, :, :, :], val[:, :, :, :], ACT.Sqrt).then_inc(rooted, 1)

        @block.tensor
        def _(pe):
            pe.wait_ge(styled, 1)
            for c in range(5):
                pe.wait_ge(squared, c + 1)
                at_least(pe, copied, c - 1)
                for k in range(KD):
                    half = k if c < 3 else KD + k
                    last = pe.matmul(pd[c % 2][0:B, :], cond2[:, half, :], sq[:, c % 2, k, :], start=k == 0, stop=k == KD - 1)
                last.then_inc(summed, 1)
                pe.wait_ge(copied, c + 1)
                at_least(pe, kept, c - 1)
                for k in range(KD):
                    last = pe.transpose(pt[c % 2][:, k * B:(k + 1) * B], rows[:, c % 2, k * P:(k + 1) * P], ident[:, :])
                last.then_inc(turned, 1)

        @block.vector
        def _(dve):
            dve.wait_ge(const, 32)
            dve.tensor_copy(s1[:, :, :], cond[:, 0:KD, :]).then_inc(kept, 1)
            for c in range(5):
                dve.wait_ge(summed, c + 1)
                at_least(dve, turned, c - 1)
                dve.tensor_copy(rows[:, c % 2, :], pd[c % 2][0:B, :]).then_inc(copied, 1)
                dve.wait_ge(turned, c + 1)
                dve.tensor_scalar(val[:, c, :, :], pt[c % 2][:, 0:KD * B].rearrange("p (k b) -> p k b", k=KD),
                                  DEMOD_EPS, None, ALU.add).then_inc(kept, 1)
            count = [0]

            def chain(ins):
                count[0] += 1
                ins.then_inc(step, 1)
                dve.wait_ge(step, count[0])

            dve.wait_ge(kept, 6)
            dve.wait_ge(rooted, 1)
            chain(dve.reciprocal(root[:, :, :, :], root[:, :, :, :]))
            chain(dve.tensor_tensor(tmp[:, :, :, :], root[:, :, :, :], root[:, :, :, :], ALU.mult))
            chain(dve.tensor_tensor(tmp[:, :, :, :], tmp[:, :, :, :], val[:, :, :, :], ALU.mult))
            chain(dve.tensor_scalar(tmp[:, :, :, :], tmp[:, :, :, :], -0.5, 1.5, ALU.mult, ALU.add))
            chain(dve.tensor_tensor(dc[:, :, :, :], tmp[:, :, :, :], root[:, :, :, :], ALU.mult))
            chain(dve.tensor_tensor(dc[:, 0, :, :], dc[:, 0, :, :], dc[:, 1, :, :], ALU.mult))
            chain(dve.tensor_scalar(dc[:, 0, :, :], dc[:, 0, :, :], float(DH) ** -0.5, None, ALU.mult))
            chain(dve.tensor_tensor(dc[:, 2, :, :], dc[:, 2, :, :], cond[:, KD:2 * KD, :], ALU.mult))


def heads_phase(nc, tag, x_in, w, cst, dram, dc, s1):
    with Phase(nc, tag) as ph:
        wh = [ph.sb(f"wh{c}", [P, KD, DM], F32R) for c in range(3)]
        wl = [ph.sb(f"wl{c}", [P, KD, DM], F32R) for c in range(3)]
        views = [w[c + "T"].rearrange("(k p) n -> p k n", p=P) for c in "qkv"]
        split_weights(nc, tag + "w", [(views[c][:, k, :], wh[c][:, k, :], wl[c][:, k, :])
                                      for c in range(3) for k in range(KD)])
        ident = ph.sb("ident", [P, P])
        ones = ph.sb("ones", [P, P])
        mean_w = ph.sb("mean_w", [P, P])
        mhalf = ph.sb("mhalf", [P, TB])
        xs = ph.sb("xs", [P, KD, TW])
        sq = ph.sb("sq", [P, KD, TW])
        xh = ph.sb("xh", [P, 2, KD, TW], F32R)
        xl = ph.sb("xl", [P, 2, KD, TW], F32R)
        vrow = ph.sb("vrow", [1, TW])
        vcol = ph.sb("vcol", [P, TB])
        rcol = ph.sb("rcol", [P, TB])
        diag = ph.sb("diag", [P, TB, S])
        qt = ph.sb("qt", [P, TW])
        qh = ph.sb("qh", [P, 2, TW], F32R)
        ql = ph.sb("ql", [P, 2, TW], F32R)
        kh = ph.sb("kh", [P, 2, TB, HG, S], F32R)
        kl = ph.sb("kl", [P, 2, TB, HG, S], F32R)
        vt = ph.sb("vt", [P, 2, TW])
        v = ph.sb("v", [P, 2, TB, DM])
        mx = ph.sb("mx", [P, 2, HG])
        e = ph.sb("e", [P, 4, HG, S])
        pt = ph.sb("pt", [P, 2, HG, S])
        rec = ph.sb("rec", [P, 2 * S])
        o = ph.sb("o", [P, 2, TW])
        ps_s = [ph.ps(f"s{k}") for k in range(2)]
        ps_p = [ph.ps(f"p{k}") for k in range(2)]
        ps_o = [ph.ps(f"o{k}") for k in range(2)]
        ps_t, ps_n = ph.ps("t"), ph.ps("n")
        const, x_ld, xs_ok, mean_mm, xc_ok, sq_ok, var_mm, row_ok, col_mm, col_ok, pow_ok, diag_ok, rs_mm, xn_ok, xh_ok, xl_ok = (
            ph.sem(n) for n in ("const", "x_ld", "xs_ok", "mean_mm", "xc_ok", "sq_ok", "var_mm", "row_ok", "col_mm",
                                "col_ok", "pow_ok", "diag_ok", "rs_mm", "xn_ok", "xh_ok", "xl_ok"))
        pj_mm, qt_ok, qh_ok, ql_ok, kh_ok, kl_ok, vt_ok = (ph.sem(n) for n in (
            "pj_mm", "qt_ok", "qh_ok", "ql_ok", "kh_ok", "kl_ok", "vt_ok"))
        s_mm, mx_ok, sub_ok, exp_ok, tu_mm, tv_mm, pt_ok, v_ok, pv_mm, rec_ok, o_ok = (ph.sem(n) for n in (
            "s_mm", "mx_ok", "sub_ok", "exp_ok", "tu_mm", "tv_mm", "pt_ok", "v_ok", "pv_mm", "rec_ok", "o_ok"))
        vt_st, o_st = ph.sems("vt_st", 2), ph.sems("o_st", 2)
        zeroed, setup = ph.sem("zeroed"), ph.sem("setup")
        block = ph.block()
        x_v = x_in.rearrange("(k p) n -> p k n", p=P)
        v_v = dram["v"].rearrange("(k p) n -> p k n", p=P)
        o_v = dram["o"].rearrange("(k p) n -> p k n", p=P)
        n_pairs = NT // 2
        Q, K, V = range(3)
        CHUNKS = {0: (Q, 1, 0), 1: (K, 1, 0), 4: (Q, 2, 0), 5: (K, 2, 0), 8: (Q, 3, 0), 9: (K, 3, 0),
                  10: (V, 0, 1), 11: (V, 1, 1), 12: (Q, 0, 1), 13: (K, 0, 1), 14: (V, 2, 1), 15: (V, 3, 1)}
        FIRST = [(V, 0), (V, 1), (V, 2), (V, 3), (Q, 0), (K, 0)]
        PER_TILE = len(CHUNKS)
        TURN_LAG, PV_LAG, OUT_LAG = 2, 3, 4

        ORDER = sorted(CHUNKS)

        def chunk_at(u, T, q, last):
            if u not in CHUNKS:
                return None
            kind, m, ahead = CHUNKS[u]
            if ahead and last and q == 1:
                return None
            at = ORDER.index(u)
            before, m_before, ahead_before = CHUNKS[ORDER[at - 2]]
            t_before = T + ahead_before - (at < 2)
            if at < 2 and isinstance(T, int) and T == 0:
                (before, m_before), t_before = FIRST[at - 2], 0
            return kind, m, T + ahead, (q + ahead) % 2, len(FIRST) + PER_TILE * T + at, at % 2, (before, m_before, t_before)

        def first_chunks():
            return [(kind, m, 0, 0, n, n % 2, FIRST[n - 2] + (0,) if n >= 2 else None)
                    for n, (kind, m) in enumerate(FIRST)]

        def lagged(T, q, u, lag, first):
            if u >= lag:
                return (T, q, u - lag) if u - lag < UNITS else None
            return None if first and q == 0 else (T - 1, 1 - q, u - lag + UNITS)

        def v_turns_before(T, u, first, q):
            if first and q == 0 and u < 13:
                return 4
            return KD * T + (2 if u == 0 else 3 if u == 1 else 4 if u < 13 else 5 if u == 13 else 6)

        def v_turn_at(u, T, q, first, last):
            if u in (0, 1) and not (first and q == 0):
                return T, q, 2 + u
            if u in (12, 13) and not (last and q == 1):
                return T + 1, 1 - q, u - 12
            return None

        DRAIN = range(UNITS, UNITS + OUT_LAG + 2)

        @block.sync
        def _(sp):
            sp.dma_start(ident[:, :], cst["ident"]).then_inc(const, 16)

            def load(T):
                at_least(sp, xl_ok, T)
                sp.dma_start(xs[:, :, :], x_v[:, :, bass.ds(T * TW, TW)]).then_inc(x_ld, 16)

            def store_v(T, m):
                n = KD * T + m
                sp.wait_ge(vt_ok, n + 1)
                sp.dma_start(v_v[:, m, bass.ds(T * TW, TW)], vt[:, m % 2, :]).then_inc(vt_st[m % 2], 16)

            def store_o(T, hg):
                sp.wait_ge(o_ok, 2 * (NG * T + hg + 1))
                sp.dma_start(o_v[:, hg, bass.ds(T * TW, TW)], o[:, hg % 2, :]).then_inc(o_st[hg % 2], 16)

            def out_slot(at):
                if at and at[2] % TB == TB - 1:
                    store_o(at[0], at[2] // TB)

            load(0)
            for m in range(KD):
                store_v(0, m)

            def body(i, first, last):
                for q in range(2):
                    T = 2 * i + q
                    for u in range(UNITS):
                        if u == 0 and not (last and q == 1):
                            load(T + 1)
                        c = chunk_at(u, T, q, last)
                        if c and c[0] == V:
                            store_v(c[2], c[1])
                        out_slot(lagged(T, q, u, OUT_LAG + 1, first))

            pairs(sp, n_pairs, body)
            for u in DRAIN:
                out_slot(lagged(NT - 1, 1, u, OUT_LAG + 1, False))
            for r in range(2):
                sp.wait_ge(vt_st[r], 16 * NT * KD // 2)
                sp.wait_ge(o_st[r], 16 * NT * NG // 2)

        @block.tensor
        def _(pe):
            pe.wait_ge(const, 16)
            pe.wait_ge(setup, 3)

            def chunk(c):
                kind, m, T, q, n, bank, before = c
                if m == 0:
                    pe.wait_ge(xl_ok, T + 1)
                if before:
                    k0, m0, T0 = before
                    done, each = ((qt_ok, 1), (kl_ok, HG), (vt_ok, 1))[k0]
                    pe.wait_ge(done, each * (KD * T0 + m0 + 1))
                for k in range(KD):
                    last = mm3(pe, ps_p[bank][:, :], wh[kind][:, k, m * P:(m + 1) * P], wl[kind][:, k, m * P:(m + 1) * P],
                               xh[:, q, k, :], xl[:, q, k, :], k == 0, k == KD - 1)
                last.then_inc(pj_mm, 1)

            def v_turn(at, unit_turns):
                T, q, m = at
                pe.wait_ge(vt_ok, KD * T + m + 1)
                at_least(pe, pt_ok, unit_turns)
                at_least(pe, v_ok, KD * T + m)
                for b in range(TB):
                    last = pe.transpose(ps_t[:, b * S:(b + 1) * S], vt[:, m % 2, b * S:(b + 1) * S], ident[:, :])
                last.then_inc(tv_mm, 1)

            def norm(T, step):
                if step == 0:
                    pe.wait_ge(xs_ok, KD * (T + 1))
                    at_least(pe, xn_ok, KD * T)
                    for k in range(KD):
                        last = pe.matmul(ps_n[:, :], mean_w[:, :], xs[:, k, :], start=k == 0, stop=k == KD - 1)
                    last.then_inc(mean_mm, 1)
                elif step == 1:
                    pe.wait_ge(sq_ok, T + 1)
                    for k in range(KD):
                        last = pe.matmul(ps_n[:, :], mean_w[:, :], sq[:, k, :], start=k == 0, stop=k == KD - 1)
                    last.then_inc(var_mm, 1)
                elif step == 2:
                    pe.wait_ge(row_ok, T + 1)
                    for b in range(TB):
                        last = pe.matmul(ps_n[:, b:b + 1], vrow[:, b * S:(b + 1) * S], ones[0:1, 0:1], start=True, stop=True)
                    last.then_inc(col_mm, 1)
                else:
                    pe.wait_ge(diag_ok, TB * (T + 1))
                    pe.matmul(ps_n[:, :], ones[:, :], diag[:, :, :].rearrange("p b s -> p (b s)"), start=True, stop=True)\
                        .then_inc(rs_mm, 1)

            def scores(T, q, u):
                hg, b = u // TB, u % TB
                g = UNITS * T + u
                if b == 0:
                    pe.wait_ge(ql_ok, NG * T + hg + 1)
                    pe.wait_ge(kl_ok, HG * (NG * T + hg + 1))
                at_least(pe, sub_ok, g - 1)
                mm3(pe, ps_s[u % 2][:, :], qh[:, hg % 2, b * S:(b + 1) * S], ql[:, hg % 2, b * S:(b + 1) * S],
                    kh[:, hg % 2, b, :, :].rearrange("p h s -> p (h s)"),
                    kl[:, hg % 2, b, :, :].rearrange("p h s -> p (h s)"), True, True).then_inc(s_mm, 1)

            def turn(at, v_turns):
                T, q, u = at
                g = UNITS * T + u
                pe.wait_ge(exp_ok, g + 1)
                at_least(pe, pt_ok, g)
                at_least(pe, v_ok, v_turns)
                for h in range(HG):
                    last = pe.transpose(ps_t[:, h * S:(h + 1) * S], e[:, u % 4, h, :], ident[:, :])
                last.then_inc(tu_mm, 1)

            def values(at):
                T, q, u = at
                hg, b = u // TB, u % TB
                g = UNITS * T + u
                pe.wait_ge(pt_ok, g + 1)
                if b == 0:
                    pe.wait_ge(v_ok, KD * T + hg + 1)
                if b % 2 == 0:
                    at_least(pe, o_ok, UNITS // 2 * T + u // 2 - 1)
                bank = ps_o[(u // 2) % 2]
                c = (b % 2) * S
                for h in range(HG):
                    pe.matmul(bank[h * DH:(h + 1) * DH, c:c + S], v[:, q, b, (hg * HG + h) * DH:(hg * HG + h + 1) * DH],
                              pt[:, u % 2, h, :], start=True, stop=True)
                for h in range(HG):
                    last = pe.matmul(bank[h * DH:(h + 1) * DH, 2 * S + c:3 * S + c], ones[:, 0:DH],
                                     pt[:, u % 2, h, :], start=True, stop=True)
                last.then_inc(pv_mm, 1)

            for step in range(4):
                norm(0, step)
            for c in first_chunks():
                chunk(c)
                if c[0] == V and c[1]:
                    v_turn((0, 0, c[1] - 1), 0)
                elif c[0] == Q:
                    v_turn((0, 0, KD - 1), 0)

            def slot(T, q, u, first, last):
                if u < UNITS:
                    scores(T, q, u)
                    c = chunk_at(u, T, q, last)
                    if c:
                        chunk(c)
                    if u in (2, 4, 5, 7) and not (last and q == 1):
                        norm(T + 1, (2, 4, 5, 7).index(u))
                at = lagged(T, q, u, TURN_LAG, first)
                turns = v_turns_before(T, u, first, q) if not (last and q == 1 and u >= 13) else KD * T + 4
                if at:
                    turn(at, turns)
                vt_at = v_turn_at(u, T, q, first, last)
                if vt_at:
                    v_turn(vt_at, UNITS * T + u + 1 - TURN_LAG)
                at = lagged(T, q, u, PV_LAG, first)
                if at:
                    values(at)

            def body(i, first, last):
                for q in range(2):
                    for u in range(UNITS):
                        slot(2 * i + q, q, u, first, last)

            pairs(pe, n_pairs, body)
            for u in DRAIN:
                slot(NT - 1, 1, u, False, True)

        @block.scalar
        def _(act):
            def chunk(c):
                kind, m, T, q, n, bank, before = c
                if kind == Q:
                    act.wait_ge(qt_ok, NG * T + m + 1)
                    at_least(act, s_mm, UNITS * T + TB * (m - 1))
                    act.activation(qh[:, m % 2, :], qt[:, :], ACT.Copy).then_inc(qh_ok, 1)
                elif kind == K:
                    act.wait_ge(pj_mm, n + 1)
                    at_least(act, s_mm, UNITS * T + TB * (m - 1))
                    for h in range(HG):
                        r = slice(h * DH, (h + 1) * DH)
                        last = act.activation(kh[r, m % 2, :, h, :], ps_p[bank][r, :].rearrange("p (b s) -> p b s", b=TB),
                                              ACT.Copy)
                        last.then_inc(kh_ok, 1)

            def keep_v(at):
                T, q, m = at
                act.wait_ge(tv_mm, KD * T + m + 1)
                at_least(act, pv_mm, UNITS * (T - 1))
                act.activation(v[:, q, :, m * P:(m + 1) * P], ps_t[:, :].rearrange("p (b s) -> p b s", b=TB), ACT.Copy)\
                    .then_inc(v_ok, 1)

            def norm(T, q, step):
                if step == 0:
                    act.wait_ge(xc_ok, KD * (T + 1))
                    at_least(act, var_mm, T)
                    act.activation(sq[:, :, :], xs[:, :, :], ACT.Square).then_inc(sq_ok, 1)
                else:
                    act.wait_ge(xn_ok, KD * (T + 1))
                    at_least(act, pj_mm, len(FIRST) + PER_TILE * (T - 2) + 6)
                    act.activation(xh[:, q, :, :], xs[:, :, :], ACT.Copy).then_inc(xh_ok, 1)

            act.wait_ge(zeroed, 2)
            norm(0, 0, 0)
            norm(0, 0, 1)
            for c in first_chunks():
                chunk(c)
                if c[0] == V and c[1]:
                    keep_v((0, 0, c[1] - 1))
                elif c[0] == Q:
                    keep_v((0, 0, KD - 1))

            def slot(T, q, u, first, last):
                if u < UNITS:
                    g = UNITS * T + u
                    act.wait_ge(sub_ok, g + 1)
                    act.activation(e[:, u % 4, :, :], e[:, u % 4, :, :], ACT.Exp).then_inc(exp_ok, 1)
                    c = chunk_at(u, T, q, last)
                    if c:
                        chunk(c)
                    if u in (3, 8) and not (last and q == 1):
                        norm(T + 1, 1 - q, (3, 8).index(u))
                at = lagged(T, q, u, TURN_LAG, first)
                if at:
                    g = UNITS * at[0] + at[2]
                    act.wait_ge(tu_mm, g + 1)
                    at_least(act, pv_mm, g - 1)
                    act.activation(pt[:, at[2] % 2, :, :], ps_t[:, :].rearrange("p (h s) -> p h s", h=HG), ACT.Copy)\
                        .then_inc(pt_ok, 1)
                vt_at = v_turn_at(u, T, q, first, last)
                if vt_at:
                    keep_v(vt_at)

            def body(i, first, last):
                for q in range(2):
                    for u in range(UNITS):
                        slot(2 * i + q, q, u, first, last)

            pairs(act, n_pairs, body)
            for u in DRAIN:
                slot(NT - 1, 1, u, False, True)

        @block.vector
        def _(dve):
            dve.memset(kh[:, :, :, :, :].bitcast(F32), 0.0).then_inc(zeroed, 1)
            dve.memset(kl[:, :, :, :, :].bitcast(F32), 0.0).then_inc(zeroed, 1)
            dve.memset(ones[:, :], 1.0).then_inc(setup, 1)
            dve.memset(mean_w[:, :], 1.0 / DM).then_inc(setup, 1)
            dve.memset(mhalf[:, :], -0.5).then_inc(setup, 1)
            dve.wait_ge(setup, 3)
            dve.wait_ge(const, 16)
            dve.wait_ge(zeroed, 2)

            def per_batch(c, m, T):
                return dc[:, c, m, bass.ds(T * TB, TB)].unsqueeze(2).to_broadcast([P, TB, S])

            def chunk(c):
                kind, m, T, q, n, bank, before = c
                src = ps_p[bank]
                if kind == K:
                    at_least(dve, s_mm, UNITS * T + TB * (m - 1))
                    for h in range(HG):
                        dve.wait_ge(kh_ok, HG * (NG * T + m) + h + 1)
                        r = slice(h * DH, (h + 1) * DH)
                        last = dve.tensor_tensor(kl[r, m % 2, :, h, :], src[r, :].rearrange("p (b s) -> p b s", b=TB),
                                                 kh[r, m % 2, :, h, :].bitcast(F32), ALU.subtract)
                        last.then_inc(kl_ok, 1)
                else:
                    dve.wait_ge(pj_mm, n + 1)
                    if kind == Q:
                        at_least(dve, ql_ok, NG * T + m)
                        dve.tensor_tensor(qt[:, :].rearrange("p (b s) -> p b s", b=TB),
                                          src[:, :].rearrange("p (b s) -> p b s", b=TB), per_batch(0, m, T), ALU.mult)\
                            .then_inc(qt_ok, 1)
                    else:
                        at_least(dve, vt_st[m % 2], 16 * (KD // 2 * T + m // 2))
                        at_least(dve, tv_mm, KD * T + m - 1)
                        dve.tensor_tensor(vt[:, m % 2, :].rearrange("p (b s) -> p b s", b=TB),
                                          src[:, :].rearrange("p (b s) -> p b s", b=TB), per_batch(2, m, T), ALU.mult)\
                            .then_inc(vt_ok, 1)

            def norm(T, q, step):
                if step == 0:
                    dve.wait_ge(mean_mm, T + 1)
                    for k in range(KD):
                        dve.tensor_tensor(xs[:, k, :], xs[:, k, :], ps_n[:, :], ALU.subtract).then_inc(xc_ok, 1)
                elif step == 1:
                    dve.wait_ge(var_mm, T + 1)
                    dve.tensor_scalar(vrow[:, :], ps_n[0:1, :], LN_EPS, None, ALU.add).then_inc(row_ok, 1)
                elif step == 2:
                    dve.wait_ge(col_mm, T + 1)
                    dve.tensor_copy(vcol[:, :], ps_n[:, 0:TB]).then_inc(col_ok, 1)
                elif step == 3:
                    dve.wait_ge(pow_ok, T + 1)
                    for b in range(TB):
                        dve.tensor_scalar(diag[:, b, :], ident[:, :], rcol[:, b:b + 1], None, ALU.mult).then_inc(diag_ok, 1)
                else:
                    dve.wait_ge(rs_mm, T + 1)
                    dve.wait_ge(xc_ok, KD * (T + 1))
                    dve.wait_ge(sq_ok, T + 1)
                    for k in range(KD):
                        dve.tensor_tensor(xs[:, k, :], xs[:, k, :], ps_n[:, :], ALU.mult).then_inc(xn_ok, 1)

            for step in range(5):
                norm(0, 0, step)
            for c in first_chunks():
                chunk(c)

            def softmax(T, q, u):
                g = UNITS * T + u
                shape = [P, HG, S]
                src = ps_s[u % 2][:, :].rearrange("p (h s) -> p h s", h=HG)
                dve.wait_ge(s_mm, g + 1)
                at_least(dve, sub_ok, g - 1)
                dve.reduce_max(mx[:, u % 2, :], src, AX.X).then_inc(mx_ok, 1)
                dve.wait_ge(mx_ok, g + 1)
                at_least(dve, tu_mm, g - 3)
                dve.tensor_tensor(e[:, u % 4, :, :], src, mx[:, u % 2, :].unsqueeze(2).to_broadcast(shape), ALU.subtract)\
                    .then_inc(sub_ok, 1)

            def finish(at):
                T, q, u = at
                hg, b = u // TB, u % TB
                pair = UNITS // 2 * T + u // 2
                dve.wait_ge(pv_mm, UNITS * T + u + 1)
                bank = ps_o[(u // 2) % 2]
                at_least(dve, o_ok, pair)
                dve.reciprocal(rec[:, :], bank[:, 2 * S:4 * S]).then_inc(rec_ok, 1)
                dve.wait_ge(rec_ok, pair + 1)
                if b == 1:
                    at_least(dve, o_st[hg % 2], 16 * (NG // 2 * T + hg // 2))
                dve.tensor_tensor(o[:, hg % 2, (b - 1) * S:(b + 1) * S], bank[:, 0:2 * S], rec[:, :], ALU.mult)\
                    .then_inc(o_ok, 1)

            def slot(T, q, u, first, last):
                if u < UNITS:
                    softmax(T, q, u)
                    c = chunk_at(u, T, q, last)
                    if c:
                        chunk(c)
                    if u in (3, 5, 6, 7, 8) and not (last and q == 1):
                        norm(T + 1, 1 - q, (3, 5, 6, 7, 8).index(u))
                at = lagged(T, q, u, OUT_LAG, first)
                if at and at[2] % 2:
                    finish(at)

            def body(i, first, last):
                for q in range(2):
                    for u in range(UNITS):
                        slot(2 * i + q, q, u, first, last)

            pairs(dve, n_pairs, body)
            for u in DRAIN:
                slot(NT - 1, 1, u, False, True)

        @block.gpsimd
        def _(pool):
            pool.wait_ge(setup, 3)

            def norm(T, q, step):
                if step == 0:
                    pool.wait_ge(x_ld, 16 * (T + 1))
                    for k in range(KD):
                        scale = s1[:, k, bass.ds(T * TB, TB)].unsqueeze(2).to_broadcast([P, TB, S])
                        view = xs[:, k, :].rearrange("p (b s) -> p b s", b=TB)
                        pool.tensor_tensor(view, view, scale, ALU.mult).then_inc(xs_ok, 1)
                elif step == 1:
                    pool.wait_ge(col_ok, T + 1)
                    at_least(pool, diag_ok, TB * T)
                    pool.tensor_tensor(rcol[:, :], vcol[:, :], mhalf[:, :], ALU.pow).then_inc(pow_ok, 1)
                else:
                    pool.wait_ge(xh_ok, T + 1)
                    pool.tensor_tensor(xl[:, q, :, :], xs[:, :, :], xh[:, q, :, :].bitcast(F32), ALU.subtract)\
                        .then_inc(xl_ok, 1)

            def chunk(c):
                kind, m, T, q, n, bank, before = c
                if kind == Q:
                    pool.wait_ge(qh_ok, NG * T + m + 1)
                    pool.tensor_tensor(ql[:, m % 2, :], qt[:, :], qh[:, m % 2, :].bitcast(F32), ALU.subtract)\
                        .then_inc(ql_ok, 1)

            for step in range(3):
                norm(0, 0, step)
            for c in first_chunks():
                chunk(c)

            def body(i, first, last):
                for q in range(2):
                    T = 2 * i + q
                    for u in range(UNITS):
                        c = chunk_at(u, T, q, last)
                        if c:
                            chunk(c)
                        if u in (1, 6, 8) and not (last and q == 1):
                            norm(T + 1, 1 - q, (1, 6, 8).index(u))

            pairs(pool, n_pairs, body)


def mix_phase(nc, tag, x_in, x_out, w, cst, dram, dc):
    with Phase(nc, tag) as ph:
        wh = [ph.sb(f"wh{c}", [P, KD, DM], F32R) for c in range(2)]
        wl = [ph.sb(f"wl{c}", [P, KD, DM], F32R) for c in range(2)]
        views = [w[c + "T"].rearrange("(k p) n -> p k n", p=P) for c in "wu"]
        split_weights(nc, tag + "w", [(views[c][:, k, :], wh[c][:, k, :], wl[c][:, k, :])
                                      for c in range(2) for k in range(KD)])
        xt = ph.sb("xt", [P, 2, KD, TW])
        src = ph.sb("src", [P, 2, KD, TW])
        hi = ph.sb("hi", [P, 2, 2, KD, TW], F32R)
        lo = ph.sb("lo", [P, 2, 2, KD, TW], F32R)
        t = ph.sb("t", [P, 2, TW])
        ps = [ph.ps(f"ps{k}") for k in range(4)]
        s_ld, x_ld, x_st = ph.sems("s_ld", 2), ph.sems("x_ld", 2), ph.sems("x_st", 2)
        high, low, mm, scaled, added = (ph.sem(n) for n in ("high", "low", "mm", "scaled", "added"))
        block = ph.block()
        x_v, y_v, v_v, o_v = (a.rearrange("(k p) n -> p k n", p=P) for a in (x_in, x_out, dram["v"], dram["o"]))
        n_pairs = NT // 2
        NC = 2 * KD

        @block.sync
        def _(sp):
            def load(T, q, uses):
                cols = bass.ds(T * TW, TW)
                for c, a in enumerate((o_v, v_v)):
                    at_least(sp, low, 2 * (T - 1) + c + 1)
                    sp.dma_start(src[:, c, :, :], a[:, :, cols]).then_inc(s_ld[c], 16)
                at_least(sp, x_st[q], 16 * uses)
                sp.dma_start(xt[:, q, :, :], x_v[:, :, cols]).then_inc(x_ld[q], 16)

            def store(T, q):
                sp.wait_ge(added, NC * (T + 1))
                sp.dma_start(y_v[:, :, bass.ds(T * TW, TW)], xt[:, q, :, :]).then_inc(x_st[q], 16)

            def body(i, first, last):
                for q in range(2):
                    T = 2 * i + q
                    if first and q == 0:
                        load(0, 0, 0)
                    if not (first and q == 0):
                        store(T - 1, 1 - q)
                    if not (last and q == 1):
                        load(T + 1, 1 - q, i + q)

            pairs(sp, n_pairs, body)
            store(NT - 1, 1)
            for q in range(2):
                sp.wait_ge(x_st[q], 16 * n_pairs)

        @block.scalar
        def _(act):
            def split(T, q):
                for c in range(2):
                    act.wait_ge(s_ld[c], 16 * (T + 1))
                    at_least(act, mm, NC * (T - 1))
                    act.activation(hi[:, q, c, :, :], src[:, c, :, :], ACT.Copy).then_inc(high, 1)

            def body(i, first, last):
                for q in range(2):
                    split(2 * i + q, q)

            pairs(act, n_pairs, body)

        @block.tensor
        def _(pe):
            def body(i, first, last):
                for q in range(2):
                    T = 2 * i + q
                    for m in range(KD):
                        for c in range(2):
                            n = NC * T + 2 * m + c
                            if m == 0:
                                pe.wait_ge(low, 2 * T + c + 1)
                            at_least(pe, scaled, n - 3)
                            for k in range(KD):
                                last_mm = mm3(pe, ps[(2 * m + c) % 4][:, :], wh[c][:, k, m * P:(m + 1) * P],
                                              wl[c][:, k, m * P:(m + 1) * P], hi[:, q, c, k, :], lo[:, q, c, k, :],
                                              k == 0, k == KD - 1)
                            last_mm.then_inc(mm, 1)

            pairs(pe, n_pairs, body)

        @block.vector
        def _(dve):
            def split(T, q):
                for c in range(2):
                    dve.wait_ge(high, 2 * T + c + 1)
                    dve.tensor_tensor(lo[:, q, c, :, :], src[:, c, :, :], hi[:, q, c, :, :].bitcast(F32), ALU.subtract)\
                        .then_inc(low, 1)

            def body(i, first, last):
                for q in range(2):
                    T = 2 * i + q
                    if first and q == 0:
                        split(0, 0)
                    for m in range(KD):
                        for c in range(2):
                            n = NC * T + 2 * m + c
                            dve.wait_ge(mm, n + 1)
                            at_least(dve, added, n - 1)
                            scale = dc[:, 3 + c, m, bass.ds(T * TB, TB)].unsqueeze(2).to_broadcast([P, TB, S])
                            dve.tensor_tensor(t[:, c, :].rearrange("p (b s) -> p b s", b=TB),
                                              ps[(2 * m + c) % 4][:, :].rearrange("p (b s) -> p b s", b=TB),
                                              scale, ALU.mult).then_inc(scaled, 1)
                        if m == 1 and not (last and q == 1):
                            split(T + 1, 1 - q)

            pairs(dve, n_pairs, body)

        @block.gpsimd
        def _(pool):
            def body(i, first, last):
                for q in range(2):
                    T = 2 * i + q
                    pool.wait_ge(x_ld[q], 16 * (i + 1))
                    for m in range(KD):
                        for c in range(2):
                            n = NC * T + 2 * m + c
                            pool.wait_ge(scaled, n + 1)
                            at_least(pool, added, n)
                            pool.tensor_tensor(xt[:, q, m, :], xt[:, q, m, :], t[:, c, :], ALU.add).then_inc(added, 1)

            pairs(pool, n_pairs, body)


def build(nc, a, out, layers="0123"):
    def scratch(name, shape, dt=F32):
        return nc.dram_tensor(name, shape, dt, kind="Internal").ap()

    dram = dict(gate=scratch("gate_s", (DI, TOK)), xhl=scratch("xhl_s", (S, 2, B, DI)),
                dx=scratch("dx_s", (S, B, DI)), y=scratch("y_s", (S, B, DI)),
                v=scratch("v_s", (DM, TOK)), o=scratch("o_s", (DM, TOK)))
    cst = dict(ident=a["ident"], pick=a["pick"], ymask=a["ymask"])

    def weights(layer):
        w = {k[3:]: v for k, v in a.items() if k.startswith(f"L{layer}_")}
        w["tembT"] = w["condT"] = a["condT"]
        w["ident"] = a["ident"]
        return w

    x = a["xT"]
    for n, layer in enumerate(layers):
        y = out if n == len(layers) - 1 else scratch(f"x{layer}_s", (DM, TOK))
        (scan_layer if layer in "03" else attention_layer)(nc, f"l{layer}", x, y, weights(layer), cst, dram)
        x = y


def kernel(**inputs):
    import numpy as np
    import concourse.bacc as bacc
    from concourse.bass_utils import run_bass_kernel_spmd

    def columns(v):
        return np.ascontiguousarray(v.reshape(-1, P).T)

    a = {k: np.asarray(v) for k, v in inputs.items()}
    arrays = {"xT": a["x"].reshape(TOK, DM).T, "condT": a["cond_2048"].T}
    for layer in (0, 3):
        w = {k.split("cond_", 1)[1]: v for k, v in a.items() if k.startswith(f"L{layer}_cond_")}
        arrays.update({f"L{layer}_{k}": v for k, v in dict(
            W_inT=w["W_in"].T, W_conv=w["W_conv"], b_convT=columns(w["b_conv"]), ln_gT=columns(w["ln_g"]),
            ln_bT=columns(w["ln_b"]), ln_g=w["ln_g"], ln_b=w["ln_b"], D=w["D"], W_xprojT=w["W_xproj"].T,
            W_xproj=w["W_xproj"], W_dtT=w["W_dt"].T, b_dt=w["b_dt"], A_log=w["A_log"], W_outT=w["W_out"].T).items()})
    for layer in (1, 2):
        for k in "qkvwu":
            arrays[f"L{layer}_{k}T"] = a[f"L{layer}_cond_{k}_weight"].T
    arrays["ident"] = np.eye(P, dtype=np.float32)
    pick = np.zeros((2, GJ, GB, GJ, GB, NS), np.float32)
    ymask = np.zeros((GB, NS, TS, TS, GB), np.float32)
    for b in range(GB):
        for j in range(GJ):
            pick[:, j, b, j, b, :] = 1.0
        for t in range(TS):
            ymask[b, :, t, t, b] = 1.0
    arrays["pick"] = pick.reshape(2 * B, GJ, P)
    arrays["ymask"] = ymask.reshape(P, TS, TS * GB)
    arrays = {k: np.ascontiguousarray(v) for k, v in arrays.items()}
    arrays = {k: v for k, v in arrays.items() if not k.startswith("L") or k[1] in LAYERS}

    nc = bacc.Bacc("TRN2", target_bir_lowering=False, num_devices=1)
    aps = {k: nc.dram_tensor(k, v.shape, F32, kind="ExternalInput").ap() for k, v in arrays.items()}
    out = nc.dram_tensor("outT", (DM, TOK), F32, kind="ExternalOutput").ap()
    build(nc, aps, out, LAYERS)
    r = run_bass_kernel_spmd(nc, [arrays], core_ids=[0])
    return np.ascontiguousarray(r.results[0]["outT"].T).reshape(B, S, DM)
LAYERS = "0123"
```

```python
import concourse.bass as bass
from concourse import mybir
from contextlib import ExitStack

F32 = mybir.dt.float32
F32R = mybir.dt.float32r
ALU = mybir.AluOpType
ACT = mybir.ActivationFunctionType
AX = mybir.AxisListType

P = 128
B, S, DM = 32, 128, 512
TOK = B * S
DI, NS = 1024, 16
KD, KI = DM // P, DI // P
TB = 4
TW = TB * S
NT = TOK // TW
NPROJ = 3 * NS
LN_EPS = 1e-5
CLIP = 10.0
GJ = 4
GB = B // GJ
TS = 4
NBLK = S // TS


class Phase:

    def __init__(self, nc, tag):
        self.nc, self.tag, self.ctx, self.signals = nc, tag, ExitStack(), []

    def __enter__(self):
        self.ctx.__enter__()
        return self

    def __exit__(self, *a):
        done = self.ctx.__exit__(*a)
        if self.signals:
            self.nc.clear_and_free_semaphores(self.signals)
            self.nc.all_engine_barrier()
        return done

    def sb(self, name, shape, dt=F32):
        return self.ctx.enter_context(self.nc.sbuf_tensor(f"{self.tag}_{name}", shape, dt))

    def ps(self, name, cols=512):
        return self.ctx.enter_context(self.nc.psum_tensor(f"{self.tag}_{name}", [P, cols], F32))

    def sem(self, name):
        signal = self.nc.alloc_semaphore(f"{self.tag}_{name}")
        self.signals.append(signal)
        return signal

    def sems(self, name, n):
        return [self.sem(f"{name}{k}") for k in range(n)]

    def block(self):
        return self.ctx.enter_context(self.nc.Block())


def at_least(eng, sem, value):
    if not (isinstance(value, int) and value <= 0):
        eng.wait_ge(sem, value)


def hold(eng):
    eng.nop(nofuse=True)


def pairs(eng, n, body):
    body(0, True, False)
    with eng.Fori(1, n - 1) as i:
        body(i, False, False)
    body(n - 1, False, True)


def mm3(pe, out, wh, wl, xh, xl, first, last):
    pe.matmul(out, wh, xh, start=first, stop=False)
    pe.matmul(out, wl, xh, start=False, stop=False)
    return pe.matmul(out, wh, xl, start=False, stop=last)


def split_weights(nc, tag, parts):
    with Phase(nc, tag) as ph:
        stage = ph.sb("stage", [P, 2, 2048])
        loaded = ph.sems("loaded", 2)
        high_done, low_done = ph.sem("high"), ph.sem("low")
        block = ph.block()

        @block.sync
        def _(sp):
            for c, (src, hi, lo) in enumerate(parts):
                n = src.shape[1]
                at_least(sp, low_done, c - 1)
                sp.dma_start(stage[:, c % 2, 0:n], src).then_inc(loaded[c % 2], 16)

        @block.scalar
        def _(act):
            for c, (src, hi, lo) in enumerate(parts):
                n = src.shape[1]
                act.wait_ge(loaded[c % 2], 16 * (c // 2 + 1))
                act.activation(hi, stage[:, c % 2, 0:n], ACT.Copy).then_inc(high_done, 1)

        @block.vector
        def _(dve):
            for c, (src, hi, lo) in enumerate(parts):
                n = src.shape[1]
                dve.wait_ge(high_done, c + 1)
                dve.tensor_tensor(lo, stage[:, c % 2, 0:n], hi.bitcast(F32), ALU.subtract).then_inc(low_done, 1)


def scan_layer(nc, tag, x_in, x_out, w, cst, dram):
    with Phase(nc, tag + "s") as keep:
        proj = keep.sb("proj", [P, B, NPROJ])
        stat = keep.sb("stat", [P, B, 4])
        wsum = keep.sb("wsum", [P, NPROJ])
        wbias = keep.sb("wbias", [P, NPROJ])
        project_phase(nc, tag + "a", x_in, w, cst, dram, proj, stat, wsum, wbias)
        woh = keep.sb("woh", [P, KI, DM], F32R)
        wol = keep.sb("wol", [P, KI, DM], F32R)
        with Phase(nc, tag + "k") as keep2:
            coef = keep2.sb("coef", [P, S, 4, GJ])
            coefficient_phase(nc, tag + "b", w, cst, proj, stat, wsum, wbias, coef)
            recurrence_phase(nc, tag + "r", w, cst, dram, coef, woh, wol)
        output_phase(nc, tag + "o", x_in, x_out, cst, dram, woh, wol)


def project_phase(nc, tag, x_in, w, cst, dram, proj, stat, wsum, wbias):
    with Phase(nc, tag) as ph:
        wih = ph.sb("wih", [P, KD, 2 * DI], F32R)
        wil = ph.sb("wil", [P, KD, 2 * DI], F32R)
        w_in = w["W_inT"].rearrange("(k p) n -> p k n", p=P)
        temb = ph.sb("temb", [P, KI, B])
        wconv = ph.sb("wconv", [P, KI, 4])
        bconv = ph.sb("bconv", [P, KI])
        gcol = ph.sb("gcol", [P, KI])
        bcol = ph.sb("bcol", [P, KI])
        grow = ph.sb("grow", [P, DI])
        brow = ph.sb("brow", [P, DI])
        drow = ph.sb("drow", [P, DI])
        wxg = ph.sb("wxg", [P, KI, NPROJ])
        ident = ph.sb("ident", [P, P])
        parts = [(w_in[:, k, :], wih[:, k, :], wil[:, k, :]) for k in range(KD)]
        scan_weights(nc, tag + "p", w, cst, parts, dict(temb=temb, wconv=wconv, bconv=bconv, gcol=gcol, bcol=bcol,
                      grow=grow, brow=brow, drow=drow, wxg=wxg, ident=ident, wsum=wsum, wbias=wbias))

        xt = ph.sb("xt", [P, KD, TW])
        xh = ph.sb("xh", [P, 2, KD, TW], F32R)
        xl = ph.sb("xl", [P, 2, KD, TW], F32R)
        pad = ph.sb("pad", [P, 2, TB, S + 3])
        acc = ph.sb("acc", [P, 2, TB, S])
        xc = ph.sb("xc", [P, 2, KI, TW])
        gate = ph.sb("gate", [P, 2, TW])
        xn = ph.sb("xn", [P, 2, DI])
        xo = ph.sb("xo", [P, 2, 2, DI], F32R)
        dx = ph.sb("dx", [P, DI])
        junk = ph.sb("junk", [P, DI], mybir.dt.bfloat16)
        raw = ph.sb("raw", [NPROJ, TW])
        bst = ph.sb("bst", [P, 2, 6])
        st = ph.sb("st", [P, 2, TB, 4])
        nmr = ph.sb("nmr", [P, 2])
        veps = ph.sb("veps", [P, 2])
        mhalf = ph.sb("mhalf", [P, 1])
        pxr = [ph.ps(f"pxr{k}") for k in range(2)]
        pg = ph.ps("pg")
        ptr = [ph.ps(f"ptr{k}", 1024) for k in range(2)]
        pp = ph.ps("pp")

        x_loaded, high, low = ph.sem("x_loaded"), ph.sem("high"), ph.sem("low")
        split_used = ph.sem("split_used")
        zeroed, halved = ph.sem("zeroed"), ph.sem("halved")
        xr_mm, g_mm, p_mm, pt_mm, tr_mm = (ph.sem(n) for n in ("xr_mm", "g_mm", "p_mm", "pt_mm", "tr_mm"))
        xr_ev, tap0, taps = (ph.sem(n) for n in ("xr_ev", "tap0", "taps"))
        g_ev, xc_ev, raw_ev, proj_ev = (ph.sem(n) for n in ("g_ev", "xc_ev", "raw_ev", "proj_ev"))
        g_st = ph.sems("g_st", 2)
        bn, var, rstd, nm, z, gz, gb, dxm, xoh, ss, xol, stc = (ph.sem(n) for n in (
            "bn", "var", "rstd", "nm", "z", "gz", "gb", "dxm", "xoh", "ss", "xol", "stc"))
        xo_st, dx_st = ph.sems("xo_st", 2), ph.sem("dx_st")
        block = ph.block()
        x_v = x_in.rearrange("(k p) n -> p k n", p=P)
        gate_v = dram["gate"].rearrange("(k p) n -> p k n", p=P)
        n_pairs = NT // 2

        @block.sync
        def _(sp):
            def load(T):
                at_least(sp, low, T)
                sp.dma_start(xt[:, :, :], x_v[:, :, bass.ds(T * TW, TW)]).then_inc(x_loaded, 16)

            def store_batch(T, b):
                r = b % 2
                n = TB * T + b
                sp.wait_ge(xoh, n + 1)
                sp.wait_ge(xol, n + 1)
                sp.dma_start(dram["xhl"][:, :, bass.ds(n, 1), :].rearrange("t h b i -> t h (b i)"),
                             xo[:, r, :, :].bitcast(F32)).then_inc(xo_st[r], 16)
                sp.wait_ge(dxm, n + 1)
                sp.dma_start(dram["dx"][:, bass.ds(n, 1), :].rearrange("t b i -> t (b i)"),
                             dx[:, :]).then_inc(dx_st, 16)

            def body(i, first, last):
                for q in range(2):
                    T = 2 * i + q
                    if first and q == 0:
                        load(0)
                    for it in range(KI):
                        sp.wait_ge(g_ev, KI * T + it + 1)
                        sp.dma_start(gate_v[:, it, bass.ds(T * TW, TW)], gate[:, it % 2, :]).then_inc(g_st[it % 2], 16)
                        if it == 0 and not (last and q == 1):
                            load(T + 1)
                        if it == 1 and not first:
                            store_batch(T - 2, TB - 1)
                        if it % 2 == 1 and it > 1 and not (first and q == 0):
                            store_batch(T - 1, it // 2 - 1)

            pairs(sp, n_pairs, body)
            store_batch(NT - 2, TB - 1)
            for b in range(TB):
                store_batch(NT - 1, b)
            for r in range(2):
                sp.wait_ge(g_st[r], 16 * NT * KI // 2)
                sp.wait_ge(xo_st[r], 16 * B // 2)
            sp.wait_ge(dx_st, 16 * B)

        @block.tensor
        def _(pe):
            def project(T, it, q):
                n = KI * T + it
                if it == 0:
                    pe.wait_ge(low, T + 1)
                at_least(pe, xr_ev, n - 1)
                for k in range(KD):
                    last = mm3(pe, pxr[it % 2][:, :], wih[:, k, it * P:(it + 1) * P], wil[:, k, it * P:(it + 1) * P],
                               xh[:, q, k, :], xl[:, q, k, :], k == 0, k == KD - 1)
                last.then_inc(xr_mm, 1)
                at_least(pe, g_ev, n)
                c = DI + it * P
                for k in range(KD):
                    last = mm3(pe, pg[:, :], wih[:, k, c:c + P], wil[:, k, c:c + P],
                               xh[:, q, k, :], xl[:, q, k, :], k == 0, k == KD - 1)
                last.then_inc(g_mm, 1)

            def xproj(T, q):
                pe.wait_ge(xc_ev, KI * (T + 1))
                at_least(pe, proj_ev, T)
                for k in range(KI):
                    last = pe.matmul(pp[0:NPROJ, :], wxg[:, k, :], xc[:, q, k, :], start=k == 0, stop=k == KI - 1)
                last.then_inc(p_mm, 1)

            def xproj_turn(T):
                pe.wait_ge(raw_ev, T + 1)
                hold(pe)
                for b in range(TB):
                    last = pe.transpose(pp[:, b * NPROJ:(b + 1) * NPROJ], raw[:, b * S:(b + 1) * S],
                                        ident[0:NPROJ, 0:NPROJ])
                last.then_inc(pt_mm, 1)

            def turn(T, b, q):
                n = TB * T + b
                if b == 0:
                    pe.wait_ge(xc_ev, KI * (T + 1))
                at_least(pe, z, n - 1)
                for k in range(KI):
                    last = pe.transpose(ptr[b % 2][:, k * P:(k + 1) * P], xc[:, q, k, b * S:(b + 1) * S], ident[:, :])
                last.then_inc(tr_mm, 1)

            def body(i, first, last):
                for q in range(2):
                    T = 2 * i + q
                    for it in range(KI):
                        project(T, it, q)
                        if not (first and q == 0):
                            if it == 1:
                                xproj(T - 1, 1 - q)
                            if it == 3:
                                xproj_turn(T - 1)
                            if it % 2 == 0:
                                turn(T - 1, it // 2, 1 - q)

            pairs(pe, n_pairs, body)
            xproj(NT - 1, 1)
            xproj_turn(NT - 1)
            for b in range(TB):
                turn(NT - 1, b, 1)

        @block.scalar
        def _(act):
            def split_high(T, q):
                act.wait_ge(x_loaded, 16 * (T + 1))
                at_least(act, g_mm, KI * (T - 1))
                act.activation(xh[:, q, :, :], xt[:, :, :], ACT.Copy).then_inc(high, 1)

            def silu_conv(T, it, q):
                n = KI * T + it
                act.wait_ge(taps, 3 * (n + 1))
                if it == 0:
                    at_least(act, tr_mm, TB * (T - 1))
                act.activation(xc[:, q, it, :], acc[:, it % 2, :, :].rearrange("p b s -> p (b s)"), ACT.Silu)\
                   .then_inc(xc_ev, 1)

            def main(T, it, q):
                n = KI * T + it
                act.wait_ge(xr_ev, n + 1)
                at_least(act, xc_ev, n - 1)
                act.activation(acc[:, it % 2, :, :], pad[:, it % 2, :, 3:3 + S], ACT.Identity,
                               bias=bconv[:, it:it + 1], scale=wconv[:, it, 3:4]).then_inc(tap0, 1)
                act.wait_ge(g_mm, n + 1)
                at_least(act, g_st[it % 2], 16 * (KI // 2 * T + it // 2))
                act.activation(gate[:, it % 2, :], pg[:, :], ACT.Silu).then_inc(g_ev, 1)
                if it:
                    silu_conv(T, it - 1, q)

            def copy_raw(T):
                act.wait_ge(p_mm, T + 1)
                act.activation(raw[:, :], pp[0:NPROJ, :], ACT.Copy).then_inc(raw_ev, 1)

            def normalise(T, b, q):
                r, n = b % 2, TB * T + b
                act.wait_ge(nm, n + 1)
                at_least(act, dxm, n - 1)
                at_least(act, ss, n - 1)
                at_least(act, xol, n - 1)
                act.activation(xn[:, r, :], ptr[r][:, :], ACT.Identity, bias=nmr[:, r:r + 1],
                               scale=st[:, q, b, 2:3]).then_inc(z, 1)

            def halves(T, b, q):
                r, n = b % 2, TB * T + b
                act.wait_ge(gb, n + 1)
                at_least(act, xo_st[r], 16 * (TB // 2 * T + b // 2))
                act.activation(xo[:, r, 0, :], xn[:, r, :], ACT.Copy).then_inc(xoh, 1)
                at_least(act, ss, n)
                act.activation(junk[:, :], xn[:, r, :], ACT.Square, accum_out=st[:, q, b, 3:4]).then_inc(ss, 1)

            def body(i, first, last):
                for q in range(2):
                    T = 2 * i + q
                    if first and q == 0:
                        split_high(0, 0)
                    for it in range(KI):
                        main(T, it, q)
                        tail = not (first and q == 0)
                        if tail and it == 2:
                            copy_raw(T - 1)
                        if it == 0 and not first:
                            halves(T - 2, TB - 1, q)
                        if tail and it % 2 == 0 and it:
                            halves(T - 1, it // 2 - 1, 1 - q)
                        if tail and it % 2 == 1:
                            normalise(T - 1, it // 2, 1 - q)
                        if it == 4 and not (last and q == 1):
                            split_high(T + 1, 1 - q)
                    silu_conv(T, KI - 1, q)

            pairs(act, n_pairs, body)
            halves(NT - 2, TB - 1, 0)
            copy_raw(NT - 1)
            for b in range(TB + 1):
                if b < TB:
                    normalise(NT - 1, b, 1)
                if b:
                    halves(NT - 1, b - 1, 1)

        @block.vector
        def _(dve):
            def split_low(T, q):
                dve.wait_ge(high, T + 1)
                dve.tensor_tensor(xl[:, q, :, :], xt[:, :, :], xh[:, q, :, :].bitcast(F32), ALU.subtract)\
                   .then_inc(low, 1)

            def evacuate(T, it):
                n = KI * T + it
                dve.wait_ge(xr_mm, n + 1)
                at_least(dve, taps, 3 * (n - 1))
                at_least(dve, tap0, n - 1)
                t = temb[:, it, bass.ds(T * TB, TB)].unsqueeze(2).to_broadcast([P, TB, S])
                dve.tensor_tensor(pad[:, it % 2, :, 3:3 + S], pxr[it % 2][:, :].rearrange("p (b s) -> p b s", b=TB),
                                  t, ALU.add).then_inc(xr_ev, 1)

            def add_taps(T, it):
                n = KI * T + it
                dve.wait_ge(tap0, n + 1)
                dve.wait_ge(xr_ev, n + 1)
                for c in range(3):
                    a = acc[:, it % 2, :, :]
                    if c:
                        dve.wait_ge(taps, 3 * n + c)
                    done = dve.scalar_tensor_tensor(out=a, in0=pad[:, it % 2, :, c:c + S], scalar=wconv[:, it, c:c + 1],
                                                    in1=a, op0=ALU.mult, op1=ALU.add)
                    done.then_inc(taps, 1)

            def statistics(T, b, q):
                n = TB * T + b
                dve.wait_ge(tr_mm, n + 1)
                at_least(dve, bn, 3 * n)
                dve.bn_stats(bst[:, 0, :], ptr[b % 2][:, 0:512]).then_inc(bn, 1)
                dve.bn_stats(bst[:, 1, :], ptr[b % 2][:, 512:1024]).then_inc(bn, 1)
                dve.wait_ge(bn, 3 * n + 2)
                if b == 0:
                    at_least(dve, stc, T - 1)
                hold(dve)
                dve.bn_aggr(st[:, q, b, 0:2], bst[:, :, :].rearrange("p a c -> p (a c)")).then_inc(bn, 1)
                dve.wait_ge(bn, 3 * n + 3)
                at_least(dve, rstd, n - 1)
                dve.tensor_scalar(veps[:, b % 2:b % 2 + 1], st[:, q, b, 1:2], LN_EPS, None, ALU.add).then_inc(var, 1)

            def low_half(T, b):
                r, n = b % 2, TB * T + b
                dve.wait_ge(xoh, n + 1)
                dve.tensor_tensor(xo[:, r, 1, :], xn[:, r, :], xo[:, r, 0, :].bitcast(F32), ALU.subtract)\
                   .then_inc(xol, 1)

            def keep_projection(T):
                dve.wait_ge(pt_mm, T + 1)
                dve.tensor_copy(proj[:, bass.ds(T * TB, TB), :],
                                pp[:, 0:TB * NPROJ].rearrange("p (b c) -> p b c", b=TB)).then_inc(proj_ev, 1)

            def keep_statistics(T, q):
                dve.wait_ge(ss, TB * (T + 1))
                dve.tensor_copy(stat[:, bass.ds(T * TB, TB), :], st[:, q, :, :]).then_inc(stc, 1)

            dve.memset(pad[:, :, :, 0:3], 0.0).then_inc(zeroed, 1)
            dve.memset(mhalf[:, :], -0.5).then_inc(halved, 1)
            dve.wait_ge(zeroed, 1)

            def body(i, first, last):
                for q in range(2):
                    T = 2 * i + q
                    if first and q == 0:
                        split_low(0, 0)
                    evacuate(T, 0)
                    for it in range(KI):
                        if it + 1 < KI:
                            evacuate(T, it + 1)
                        add_taps(T, it)
                        tail = not (first and q == 0)
                        if it == 1 and not first:
                            low_half(T - 2, TB - 1)
                            keep_statistics(T - 2, q)
                        if tail and it == 4:
                            keep_projection(T - 1)
                        if tail and it % 2 == 1 and it > 1:
                            low_half(T - 1, it // 2 - 1)
                        if tail and it % 2 == 0:
                            statistics(T - 1, it // 2, 1 - q)
                        if it == 4 and not (last and q == 1):
                            split_low(T + 1, 1 - q)

            pairs(dve, n_pairs, body)
            low_half(NT - 2, TB - 1)
            keep_statistics(NT - 2, 0)
            for b in range(TB + 1):
                if b < TB:
                    statistics(NT - 1, b, 1)
                if b == 0:
                    keep_projection(NT - 1)
                else:
                    low_half(NT - 1, b - 1)
            keep_statistics(NT - 1, 1)

        @block.gpsimd
        def _(pool):
            pool.wait_ge(halved, 1)

            def batch(T, b, q):
                r, n = b % 2, TB * T + b
                pool.wait_ge(var, n + 1)
                pool.tensor_tensor(st[:, q, b, 2:3], veps[:, r:r + 1], mhalf[:, :], ALU.pow).then_inc(rstd, 1)
                pool.wait_ge(rstd, n + 1)
                at_least(pool, z, n - 1)
                hold(pool)
                pool.tensor_scalar(nmr[:, r:r + 1], st[:, q, b, 0:1], st[:, q, b, 2:3], -1.0, ALU.mult, ALU.mult)\
                    .then_inc(nm, 1)
                pool.wait_ge(z, n + 1)
                pool.tensor_tensor(xn[:, r, :], xn[:, r, :], grow[:, :], ALU.mult).then_inc(gz, 1)
                pool.wait_ge(gz, n + 1)
                pool.tensor_tensor(xn[:, r, :], xn[:, r, :], brow[:, :], ALU.add).then_inc(gb, 1)
                pool.wait_ge(gb, n + 1)
                at_least(pool, dx_st, 16 * n)
                pool.tensor_tensor(dx[:, :], xn[:, r, :], drow[:, :], ALU.mult).then_inc(dxm, 1)

            def body(i, first, last):
                for q in range(2):
                    if not (first and q == 0):
                        for b in range(TB):
                            batch(2 * i + q - 1, b, 1 - q)

            pairs(pool, n_pairs, body)
            for b in range(TB):
                batch(NT - 1, b, 1)


def scan_weights(nc, tag, w, cst, parts, t):
    with Phase(nc, tag) as ph:
        stage = ph.sb("stage", [P, 2, 2048])
        part_loaded = ph.sems("part_loaded", 2)
        high_done, low_done = ph.sem("high"), ph.sem("low")
        wx = ph.sb("wx", [P, KI, NPROJ])
        wxb = ph.sb("wxb", [P, KI, NPROJ])
        wxdt = ph.sb("wxdt", [NS, DI])
        wdt = ph.sb("wdt", [NS, NS])
        bdt = ph.sb("bdt", [P, NS])
        ones = ph.sb("ones", [P, P])
        pf, psum_s, psum_b = ph.ps("pf"), ph.ps("ps"), ph.ps("pb")
        loaded, folded, copied, scaled, summed, kept = (ph.sem(n) for n in (
            "loaded", "folded", "copied", "scaled", "summed", "kept"))
        block = ph.block()
        loads = [(t["temb"][:, :, :], w["tembT"].rearrange("(k p) b -> p k b", p=P)),
                 (t["wconv"][:, :, :], w["W_conv"].rearrange("(k p) a c -> p k (a c)", p=P)),
                 (t["bconv"][:, :], w["b_convT"]),
                 (t["gcol"][:, :], w["ln_gT"]), (t["bcol"][:, :], w["ln_bT"]),
                 (t["grow"][:, :], w["ln_g"].partition_broadcast(P)),
                 (t["brow"][:, :], w["ln_b"].partition_broadcast(P)),
                 (t["drow"][:, :], w["D"].partition_broadcast(P)),
                 (t["ident"][:, :], cst["ident"]),
                 (wx[:, :, :], w["W_xprojT"].rearrange("(k p) c -> p k c", p=P)),
                 (wxdt[:, :], w["W_xproj"][2 * NS:NPROJ, :]),
                 (wdt[:, :], w["W_dtT"]),
                 (bdt[:, :], w["b_dt"].partition_broadcast(P))]

        @block.sync
        def _(sp):
            for c, (src, hi, lo) in enumerate(parts):
                at_least(sp, low_done, c - 1)
                sp.dma_start(stage[:, c % 2, 0:src.shape[1]], src).then_inc(part_loaded[c % 2], 16)

        @block.scalar
        def _(act):
            for dst, src in loads:
                act.dma_start(dst, src).then_inc(loaded, 16)
            for c, (src, hi, lo) in enumerate(parts):
                act.wait_ge(part_loaded[c % 2], 16 * (c // 2 + 1))
                act.activation(hi, stage[:, c % 2, 0:src.shape[1]], ACT.Copy).then_inc(high_done, 1)

        @block.tensor
        def _(pe):
            pe.wait_ge(loaded, 16 * len(loads))
            for k in range(KI):
                last = pe.matmul(pf[:, k * NS:(k + 1) * NS], wxdt[:, k * P:(k + 1) * P], wdt[:, :], start=True, stop=True)
            last.then_inc(folded, 1)
            pe.wait_ge(scaled, 3)
            for k in range(KI):
                pe.matmul(psum_s[:, 0:NPROJ], ones[:, :], t["wxg"][:, k, :], start=k == 0, stop=k == KI - 1)
            for k in range(KI):
                last = pe.matmul(psum_b[:, 0:NPROJ], ones[:, :], wxb[:, k, :], start=k == 0, stop=k == KI - 1)
            last.then_inc(summed, 1)

        @block.vector
        def _(dve):
            dve.memset(ones[:, :], 1.0).then_inc(scaled, 1)

            def fold_gain():
                dve.wait_ge(loaded, 16 * len(loads))
                dve.wait_ge(folded, 1)
                dve.tensor_copy(wx[:, :, 2 * NS:NPROJ], pf[:, 0:KI * NS].rearrange("p (k c) -> p k c", k=KI))\
                   .then_inc(copied, 1)
                dve.wait_ge(copied, 1)
                for dst, col in ((t["wxg"], t["gcol"]), (wxb, t["bcol"])):
                    dve.tensor_tensor(dst[:, :, :], wx[:, :, :], col[:, :].unsqueeze(2).to_broadcast([P, KI, NPROJ]),
                                      ALU.mult).then_inc(scaled, 1)

            for c, (src, hi, lo) in enumerate(parts):
                if c == 2:
                    fold_gain()
                dve.wait_ge(high_done, c + 1)
                dve.tensor_tensor(lo, stage[:, c % 2, 0:src.shape[1]], hi.bitcast(F32), ALU.subtract)\
                   .then_inc(low_done, 1)
            dve.wait_ge(summed, 1)
            dve.tensor_copy(t["wsum"][:, :], psum_s[:, 0:NPROJ]).then_inc(kept, 1)
            dve.tensor_copy(t["wbias"][:, 0:2 * NS], psum_b[:, 0:2 * NS]).then_inc(kept, 1)
            dve.tensor_tensor(t["wbias"][:, 2 * NS:NPROJ], psum_b[:, 2 * NS:NPROJ], bdt[:, :], ALU.add).then_inc(kept, 1)
            dve.wait_ge(kept, 3)


def coefficient_phase(nc, tag, w, cst, proj, stat, wsum, wbias, coef):
    with Phase(nc, tag) as ph:
        ident = ph.sb("ident", [P, P])
        alog = ph.sb("alog", [P, 1])
        acol = ph.sb("acol", [P, 2])
        half = ph.sb("half", [P, 1])
        mean_w = ph.sb("mean_w", [P, B, NPROJ])
        norm = ph.sb("norm", [P, B])
        parts = [ph.sb(f"part{c}", [P, B, NS]) for c in range(3)]
        decay = ph.sb("decay", [P, GJ, S])
        zero = ph.sb("zero", [P, S])
        prod = ph.sb("prod", [P, GJ, S])
        inv = ph.sb("inv", [P, GJ, S])
        pt = [ph.ps(f"pt{c}") for c in range(3)]
        loaded, root, step, turned, tanh = (ph.sem(n) for n in ("loaded", "root", "step", "turned", "tanh"))
        block = ph.block()

        @block.sync
        def _(sp):
            sp.dma_start(ident[:, :], cst["ident"]).then_inc(loaded, 16)
            for b in range(GB):
                sp.dma_start(alog[b * NS:(b + 1) * NS, :], w["A_log"].rearrange("(n a) -> n a", a=1)).then_inc(loaded, 16)

        @block.gpsimd
        def _(pool):
            pool.memset(half[:, :], 0.5).then_inc(root, 1)
            pool.wait_ge(root, 1)
            pool.tensor_tensor(norm[:, :], stat[:, :, 3], half[:, :].to_broadcast([P, B]), ALU.pow).then_inc(root, 1)

        @block.vector
        def _(dve):
            count = [0]

            def chain(ins):
                count[0] += 1
                ins.then_inc(step, 1)
                dve.wait_ge(step, count[0])

            full = [P, B, NPROJ]
            chain(dve.tensor_tensor(mean_w[:, :, :], stat[:, :, 0].unsqueeze(2).to_broadcast(full),
                                    wsum[:, :].unsqueeze(1).to_broadcast(full), ALU.mult))
            chain(dve.tensor_tensor(proj[:, :, :], proj[:, :, :], mean_w[:, :, :], ALU.subtract))
            chain(dve.tensor_tensor(proj[:, :, :], proj[:, :, :], stat[:, :, 2].unsqueeze(2).to_broadcast(full), ALU.mult))
            chain(dve.tensor_tensor(proj[:, :, :], proj[:, :, :], wbias[:, :].unsqueeze(1).to_broadcast(full), ALU.add))
            dve.wait_ge(root, 2)
            chain(dve.tensor_scalar(norm[:, :], norm[:, :], 1.0, None, ALU.min))
            chain(dve.tensor_tensor(parts[0][:, :, :], proj[:, :, 0:NS], norm[:, :].unsqueeze(2).to_broadcast([P, B, NS]),
                                    ALU.mult))
            chain(dve.tensor_copy(parts[1][:, :, :], proj[:, :, NS:2 * NS]))
            chain(dve.tensor_copy(parts[2][:, :, :], proj[:, :, 2 * NS:NPROJ]))
            chain(dve.memset(zero[:, :], 0.0))
            dve.wait_ge(tanh, 2)
            chain(dve.tensor_scalar(acol[:, 1:2], acol[:, 0:1], -0.01, None, ALU.mult))
            chain(dve.tensor_scalar(decay[:, :, :], decay[:, :, :], acol[:, 1:2], 1.0, ALU.mult, ALU.add))
            for j in range(GJ):
                chain(dve.tensor_tensor_scan(prod[:, j, :], decay[:, j, :], zero[:, :], 1.0, ALU.mult, ALU.add))
            chain(dve.reciprocal(inv[:, :, :], prod[:, :, :]))
            out = [coef[:, :, c, :].rearrange("p s j -> p j s") for c in range(4)]
            chain(dve.tensor_scalar(out[0], inv[:, :, :], CLIP, None, ALU.mult))
            chain(dve.tensor_scalar(out[1], inv[:, :, :], -CLIP, None, ALU.mult))
            turn = [pt[c][:, :].rearrange("p (j s) -> p j s", j=GJ) for c in range(2)]
            dve.wait_ge(turned, 1)
            chain(dve.tensor_tensor(out[2], turn[0], inv[:, :, :], ALU.mult))
            chain(dve.tensor_tensor(out[3], turn[1], prod[:, :, :], ALU.mult))

        @block.tensor
        def _(pe):
            pe.wait_ge(loaded, 16 * (1 + GB))
            pe.wait_ge(step, 8)
            for c in range(3):
                for j in range(GJ):
                    last = pe.transpose(pt[c][:, j * S:(j + 1) * S],
                                        parts[c][:, j * GB:(j + 1) * GB, :].rearrange("p b n -> p (b n)"), ident[:, :])
            last.then_inc(turned, 1)

        @block.scalar
        def _(act):
            act.wait_ge(loaded, 16 * (1 + GB))
            act.activation(acol[:, 0:1], alog[:, :], ACT.Tanh).then_inc(tanh, 1)
            act.wait_ge(turned, 1)
            act.activation(decay[:, :, :].rearrange("p j s -> p (j s)"), pt[2][:, :], ACT.Tanh).then_inc(tanh, 1)


def recurrence_phase(nc, tag, w, cst, dram, coef, woh, wol):
    HALF = DI // 2
    with Phase(nc, tag) as ph:
        pick = ph.sb("pick", [P, 2, GJ, P], F32R)
        pickf = ph.sb("pickf", [P, 2, GJ, P])
        ymask = ph.sb("ymask", [P, TS, TS * GB])
        ident = ph.sb("ident", [P, P])
        x = ph.sb("x", [P, 2, TS // 2, DI], F32R)
        cf = ph.sb("cf", [P, 2, TS, 4, GJ])
        cd = ph.sb("cd", [P, 2, TS, GJ, TS * GB])
        v = ph.sb("v", [P, GJ, DI])
        g = ph.sb("g", [P, TS, GJ, DI])
        dxt = ph.sb("dxt", [P, 2, DI])
        y = ph.sb("y", [P, 2, DI])
        pv = [ph.ps(f"pv{k}", DI) for k in range(2)]
        py = [ph.ps(f"py{k}", DI) for k in range(2)]
        const, picked = ph.sem("const"), ph.sem("picked")
        x_ld, dx_ld, y_st = ph.sems("x_ld", 2), ph.sems("dx_ld", 2), ph.sems("y_st", 2)
        cfc, cdm, bmm, vev, gup, dmm, ymm, yad = (ph.sem(n) for n in (
            "cfc", "cdm", "bmm", "vev", "gup", "dmm", "ymm", "yad"))
        block = ph.block()
        n_pairs = NBLK // 2
        LAG = 2
        wst = ph.sb("wst", [P, KI, DM])
        w_ld, high, low = ph.sem("w_ld"), ph.sem("high"), ph.sem("low")

        @block.sync
        def _(sp):
            sp.dma_start(pickf[:, :, :, :], cst["pick"]).then_inc(const, 16)
            sp.dma_start(ymask[:, :, :], cst["ymask"]).then_inc(const, 16)
            sp.dma_start(ident[:, :], cst["ident"]).then_inc(const, 16)

            def load(k, q):
                at_least(sp, bmm, GJ * TS * (k - 1))
                sp.dma_start(x[:, q, :, :].bitcast(F32), dram["xhl"][bass.ds(k * TS, TS), :, :, :].rearrange("(s t) h b i -> (t h b) s i", t=2))\
                    .then_inc(x_ld[q], 16)
                at_least(sp, dmm, k - 1)
                for j in range(GJ):
                    sp.dma_start(dxt[j * TS * GB:(j + 1) * TS * GB, q, :],
                                 dram["dx"][bass.ds(k * TS, TS), j * GB:(j + 1) * GB, :])\
                        .then_inc(dx_ld[q], 16)

            def store(k, q):
                sp.wait_ge(yad, k + 1)
                for j in range(GJ):
                    sp.dma_start(dram["y"][bass.ds(k * TS, TS), j * GB:(j + 1) * GB, :],
                                 y[j * TS * GB:(j + 1) * TS * GB, q, :]).then_inc(y_st[q], 16)

            def body(i, first, last):
                for q in range(2):
                    k = 2 * i + q
                    if first and q == 0:
                        load(0, 0)
                    if not (last and q == 1):
                        load(k + 1, 1 - q)
                    if first and q == 1:
                        sp.dma_start(wst[:, :, :], w["W_outT"].rearrange("(k p) n -> p k n", p=P)).then_inc(w_ld, 16)
                    if not (first and q == 0):
                        store(k - 1, 1 - q)

            pairs(sp, n_pairs, body)
            store(NBLK - 1, 1)
            for q in range(2):
                sp.wait_ge(y_st[q], 16 * GJ * n_pairs)

        @block.gpsimd
        def _(pool):
            pool.wait_ge(const, 48)

            def body(i, first, last):
                for q in range(2):
                    k = 2 * i + q
                    at_least(pool, gup, GJ * (TS * (k - 1) + 1))
                    at_least(pool, vev, GJ * TS * (k - 1))
                    pool.tensor_copy(cf[:, q, :, :, :].rearrange("p t c j -> p (t c j)"),
                                     coef[:, bass.ds(k * TS, TS), :, :].rearrange("p t c j -> p (t c j)"))\
                        .then_inc(cfc, 1)
                    pool.wait_ge(cfc, k + 1)
                    at_least(pool, ymm, TS * (k - 1))
                    for t in range(TS):
                        shape = [P, GJ, TS * GB]
                        last_op = pool.tensor_tensor(cd[:, q, t, :, :], ymask[:, t, :].unsqueeze(1).to_broadcast(shape),
                                                     cf[:, q, t, 3, :].unsqueeze(2).to_broadcast(shape), ALU.mult)
                        last_op.then_inc(cdm, 1)

            pairs(pool, n_pairs, body)
            for c in range(KI):
                pool.wait_ge(high, c + 1)
                pool.tensor_tensor(wol[:, c, :], wst[:, c, :], woh[:, c, :].bitcast(F32), ALU.subtract).then_inc(low, 1)

        @block.tensor
        def _(pe):
            pe.wait_ge(picked, 1)
            pe.wait_ge(const, 48)

            def spread(s, t, q, j):
                n = GJ * s + j
                at_least(pe, vev, n - 1)
                for h in range(2):
                    last = pe.matmul(pv[j % 2][:, h * HALF:(h + 1) * HALF], pick[:, t % 2, j, :],
                                     x[:, q, t // 2, h * HALF:(h + 1) * HALF], start=True, stop=True)
                last.then_inc(bmm, 1)

            def start_sum(k, q, uses):
                at_least(pe, yad, k - 1)
                pe.wait_ge(dx_ld[q], 16 * GJ * uses)
                for h in range(2):
                    last = pe.matmul(py[q][:, h * HALF:(h + 1) * HALF], ident[:, :], dxt[:, q, h * HALF:(h + 1) * HALF],
                                     start=True, stop=False)
                last.then_inc(dmm, 1)

            def read_out(at, h):
                s, k, t, q = at
                if h == 0:
                    pe.wait_ge(gup, GJ * (s + 2))
                    pe.wait_ge(cdm, TS * k + t + 1)
                for j in range(GJ):
                    last = pe.matmul(py[q][j * TS * GB:(j + 1) * TS * GB, h * HALF:(h + 1) * HALF], cd[:, q, t, j, :],
                                     g[:, t, j, h * HALF:(h + 1) * HALF], start=False, stop=t == TS - 1)
                if h == 1:
                    last.then_inc(ymm, 1)

            def body(i, first, last):
                for q in range(2):
                    k = 2 * i + q
                    pe.wait_ge(x_ld[q], 16 * (i + 1))
                    for t in range(TS):
                        s = TS * k + t
                        if t >= LAG:
                            at = (s - LAG, k, t - LAG, q)
                        else:
                            at = None if first and q == 0 else (s - LAG, k - 1, t - LAG + TS, 1 - q)
                        if t == LAG:
                            start_sum(k, q, i + 1)
                        for j in range(GJ):
                            spread(s, t, q, j)
                            if at and j % 2:
                                read_out(at, j // 2)

            pairs(pe, n_pairs, body)
            for t in range(TS - LAG, TS):
                for h in range(2):
                    read_out((S - TS + t, NBLK - 1, t, 1), h)

        @block.scalar
        def _(act):
            act.wait_ge(const, 48)
            act.activation(pick[:, :, :, :], pickf[:, :, :, :], ACT.Copy).then_inc(picked, 1)

            def keep_y(k, q, uses):
                act.wait_ge(ymm, TS * (k + 1))
                at_least(act, y_st[q], 16 * GJ * (uses - 1))
                act.activation(y[:, q, :], py[q][:, :], ACT.Copy).then_inc(yad, 1)

            def body(i, first, last):
                for q in range(2):
                    k = 2 * i + q
                    act.wait_ge(cfc, k + 1)
                    for t in range(TS):
                        for j in range(GJ):
                            n = GJ * (TS * k + t) + j
                            act.wait_ge(bmm, n + 1)
                            at_least(act, gup, n + 1)
                            act.activation(v[:, j, :], pv[j % 2][:, :], ACT.Copy, scale=cf[:, q, t, 2, j:j + 1])\
                               .then_inc(vev, 1)
                        if t == LAG and not (first and q == 0):
                            keep_y(k - 1, 1 - q, i + q)
                        if last:
                            c = TS * q + t
                            act.wait_ge(w_ld, 16)
                            act.activation(woh[:, c, :], wst[:, c, :], ACT.Copy).then_inc(high, 1)

            pairs(act, n_pairs, body)
            keep_y(NBLK - 1, 1, n_pairs)

        @block.vector
        def _(dve):
            dve.memset(g[:, TS - 1, :, :], 0.0).then_inc(gup, GJ)

            def body(i, first, last):
                for q in range(2):
                    k = 2 * i + q
                    dve.wait_ge(cfc, k + 1)
                    for t in range(TS):
                        s = TS * k + t
                        for j in range(GJ):
                            n = GJ * s + j
                            if j == 0:
                                at_least(dve, ymm, s - TS + 1)
                            dve.wait_ge(gup, n + 1)
                            dve.wait_ge(vev, n + 1)
                            hold(dve)
                            dve._custom_dve(bass.dve_ops.TENSOR_ADD_SAT, out=g[:, t, j, :],
                                            in0=g[:, (t - 1) % TS, j, :], in1=v[:, j, :],
                                            s0=cf[:, q, t, 0, j:j + 1], s1=cf[:, q, t, 1, j:j + 1]).then_inc(gup, 1)

            pairs(dve, n_pairs, body)


def output_phase(nc, tag, x_in, x_out, cst, dram, woh, wol):
    with Phase(nc, tag) as ph:
        ident = ph.sb("ident", [P, P])
        yt = ph.sb("yt", [P, 2, TB, DI])
        gt = ph.sb("gt", [P, 2, KI, TW])
        xt = ph.sb("xt", [P, 2, KD, TW])
        zt = ph.sb("zt", [P, 2, TW])
        zh = ph.sb("zh", [P, 2, TW], F32R)
        zl = ph.sb("zl", [P, 2, TW], F32R)
        ptr = [ph.ps(f"ptr{k}") for k in range(4)]
        pout = [ph.ps(f"pout{k}") for k in range(KD)]
        const = ph.sem("const")
        y_ld, g_ld, x_ld, x_st = (ph.sems(n, 2) for n in ("y_ld", "g_ld", "x_ld", "x_st"))
        trm, gated, high, low, omm, res = (ph.sem(n) for n in ("trm", "gated", "high", "low", "omm", "res"))
        block = ph.block()
        x_v = x_in.rearrange("(k p) n -> p k n", p=P)
        o_v = x_out.rearrange("(k p) n -> p k n", p=P)
        gate_v = dram["gate"].rearrange("(k p) n -> p k n", p=P)
        n_pairs = NT // 2
        LEAD = 2

        @block.sync
        def _(sp):
            sp.dma_start(ident[:, :], cst["ident"]).then_inc(const, 16)

            def load(T, q):
                at_least(sp, trm, KI * (T - 1))
                sp.dma_start(yt[:, q, :, :], dram["y"][:, bass.ds(T * TB, TB), :]).then_inc(y_ld[q], 16)
                at_least(sp, gated, KI * (T - 1))
                sp.dma_start(gt[:, q, :, :], gate_v[:, :, bass.ds(T * TW, TW)]).then_inc(g_ld[q], 16)

            def load_x(T, q, i):
                at_least(sp, x_st[q], 16 * i)
                sp.dma_start(xt[:, q, :, :], x_v[:, :, bass.ds(T * TW, TW)]).then_inc(x_ld[q], 16)

            def store(T, q):
                sp.wait_ge(res, KD * (T + 1))
                sp.dma_start(o_v[:, :, bass.ds(T * TW, TW)], xt[:, q, :, :]).then_inc(x_st[q], 16)

            def body(i, first, last):
                for q in range(2):
                    T = 2 * i + q
                    if first and q == 0:
                        load(0, 0)
                        load_x(0, 0, 0)
                    if not (last and q == 1):
                        load(T + 1, 1 - q)
                    if not (first and q == 0):
                        store(T - 1, 1 - q)
                    if not (last and q == 1):
                        load_x(T + 1, 1 - q, i + q)

            pairs(sp, n_pairs, body)
            store(NT - 1, 1)
            for q in range(2):
                sp.wait_ge(x_st[q], 16 * n_pairs)

        @block.tensor
        def _(pe):
            pe.wait_ge(const, 16)

            def turn(T, k, q, i):
                n = KI * T + k
                if k == 0:
                    pe.wait_ge(y_ld[q], 16 * (i + 1))
                at_least(pe, gated, n - 3)
                for b in range(TB):
                    last = pe.transpose(ptr[k % 4][:, b * S:(b + 1) * S], yt[:, q, b, k * P:(k + 1) * P], ident[:, :])
                last.then_inc(trm, 1)

            def project(T, k, q):
                n = KI * T + k
                pe.wait_ge(low, n + 1)
                if k == 0:
                    at_least(pe, res, KD * T)
                for m in range(KD):
                    last = mm3(pe, pout[m][:, :], woh[:, k, m * P:(m + 1) * P], wol[:, k, m * P:(m + 1) * P],
                               zh[:, k % 2, :], zl[:, k % 2, :], k == 0, k == KI - 1)
                last.then_inc(omm, 1)

            def body(i, first, last):
                for q in range(2):
                    T = 2 * i + q
                    if first and q == 0:
                        for k in range(LEAD):
                            turn(0, k, 0, 0)
                    for k in range(KI):
                        if k + LEAD < KI:
                            turn(T, k + LEAD, q, i)
                        elif not (last and q == 1):
                            turn(T + 1, k + LEAD - KI, 1 - q, i + q)
                        project(T, k, q)

            pairs(pe, n_pairs, body)

        @block.vector
        def _(dve):
            def gating(T, k, q, i):
                n = KI * T + k
                if k == 0:
                    dve.wait_ge(g_ld[q], 16 * (i + 1))
                dve.wait_ge(trm, n + 1)
                at_least(dve, high, n - 1)
                at_least(dve, low, n - 1)
                dve.tensor_tensor(zt[:, k % 2, :], ptr[k % 4][:, :], gt[:, q, k, :], ALU.mult).then_inc(gated, 1)

            def residual(T, q, i):
                dve.wait_ge(omm, KI * (T + 1))
                dve.wait_ge(x_ld[q], 16 * (i + 1))
                for m in range(KD):
                    dve.tensor_tensor(xt[:, q, m, :], xt[:, q, m, :], pout[m][:, :], ALU.add).then_inc(res, 1)

            def body(i, first, last):
                for q in range(2):
                    T = 2 * i + q
                    for k in range(KI):
                        gating(T, k, q, i)
                        if k == 0 and not (first and q == 0):
                            residual(T - 1, 1 - q, i + q - 1)

            pairs(dve, n_pairs, body)
            residual(NT - 1, 1, n_pairs - 1)

        @block.scalar
        def _(act):
            def body(i, first, last):
                for q in range(2):
                    T = 2 * i + q
                    for k in range(KI):
                        n = KI * T + k
                        act.wait_ge(gated, n + 1)
                        at_least(act, omm, n - 1)
                        act.activation(zh[:, k % 2, :], zt[:, k % 2, :], ACT.Copy).then_inc(high, 1)

            pairs(act, n_pairs, body)

        @block.gpsimd
        def _(pool):
            def body(i, first, last):
                for q in range(2):
                    T = 2 * i + q
                    for k in range(KI):
                        n = KI * T + k
                        pool.wait_ge(high, n + 1)
                        pool.tensor_tensor(zl[:, k % 2, :], zt[:, k % 2, :],
                                           zh[:, k % 2, :].bitcast(F32), ALU.subtract).then_inc(low, 1)

            pairs(pool, n_pairs, body)


NHEAD = 16
DH = DM // NHEAD
HG = 4
NG = NHEAD // HG
UNITS = NG * TB
DEMOD_EPS = 1e-8


def attention_layer(nc, tag, x_in, x_out, w, cst, dram):
    with Phase(nc, tag + "c") as keep:
        dc = keep.sb("dc", [P, 5, KD, B])
        s1 = keep.sb("s1", [P, KD, B])
        wh = [keep.sb(f"wh{c}", [P, KD, DM], F32R) for c in range(4)]
        wl = [keep.sb(f"wl{c}", [P, KD, DM], F32R) for c in range(4)]
        demodulation_phase(nc, tag + "d", w, dc, s1, wh, wl)
        heads_phase(nc, tag + "h", x_in, w, cst, dram, dc, s1, wh[:3], wl[:3])
        mix_phase(nc, tag + "m", x_in, x_out, w, cst, dram, dc, wh[3:], wl[3:])


def demodulation_phase(nc, tag, w, dc, s1, wh, wl):
    with Phase(nc, tag) as ph:
        wt = ph.sb("wt", [P, 2, KD, DM])
        sq = ph.sb("sq", [P, 2, KD, DM])
        cond = ph.sb("cond", [P, 2 * KD, B])
        cond2 = ph.sb("cond2", [P, 2 * KD, B])
        ident = ph.sb("ident", [B, B])
        rows = ph.sb("rows", [B, 2, DM])
        val = ph.sb("val", [P, 5, KD, B])
        root = ph.sb("root", [P, 5, KD, B])
        tmp = ph.sb("tmp", [P, 5, KD, B])
        pd = [ph.ps(f"pd{k}") for k in range(2)]
        pt = [ph.ps(f"pt{k}") for k in range(2)]
        loaded, const = ph.sems("loaded", 2), ph.sem("const")
        styled, high, low, squared, summed, copied, turned, kept, rooted, step = (ph.sem(n) for n in (
            "styled", "high", "low", "squared", "summed", "copied", "turned", "kept", "rooted", "step"))
        block = ph.block()

        @block.sync
        def _(sp):
            sp.dma_start(cond[:, :, :], w["condT"].rearrange("(k p) b -> p k b", p=P)).then_inc(const, 16)
            sp.dma_start(ident[:, :], w["ident"][0:B, 0:B]).then_inc(const, 16)
            for c, name in enumerate("qkvwu"):
                at_least(sp, squared, c - 1)
                at_least(sp, low, c - 1)
                sp.dma_start(wt[:, c % 2, :, :], w[name + "T"].rearrange("(k p) n -> p k n", p=P))\
                    .then_inc(loaded[c % 2], 16)

        @block.scalar
        def _(act):
            act.wait_ge(const, 32)
            act.activation(cond2[:, :, :], cond[:, :, :], ACT.Square).then_inc(styled, 1)
            for c in range(5):
                act.wait_ge(loaded[c % 2], 16 * (c // 2 + 1))
                if c < len(wh):
                    act.activation(wh[c][:, :, :], wt[:, c % 2, :, :], ACT.Copy).then_inc(high, 1)
                at_least(act, summed, c - 1)
                act.activation(sq[:, c % 2, :, :], wt[:, c % 2, :, :], ACT.Square).then_inc(squared, 1)
            act.wait_ge(kept, 6)
            act.activation(root[:, :, :, :], val[:, :, :, :], ACT.Sqrt).then_inc(rooted, 1)

        @block.tensor
        def _(pe):
            pe.wait_ge(styled, 1)
            for c in range(5):
                pe.wait_ge(squared, c + 1)
                at_least(pe, copied, c - 1)
                for k in range(KD):
                    half = k if c < 3 else KD + k
                    last = pe.matmul(pd[c % 2][0:B, :], cond2[:, half, :], sq[:, c % 2, k, :], start=k == 0, stop=k == KD - 1)
                last.then_inc(summed, 1)
                pe.wait_ge(copied, c + 1)
                at_least(pe, kept, c - 1)
                for k in range(KD):
                    last = pe.transpose(pt[c % 2][:, k * B:(k + 1) * B], rows[:, c % 2, k * P:(k + 1) * P], ident[:, :])
                last.then_inc(turned, 1)

        @block.vector
        def _(dve):
            dve.wait_ge(const, 32)
            dve.tensor_copy(s1[:, :, :], cond[:, 0:KD, :]).then_inc(kept, 1)
            for c in range(5):
                if c < len(wh):
                    dve.wait_ge(high, c + 1)
                    dve.tensor_tensor(wl[c][:, :, :], wt[:, c % 2, :, :], wh[c][:, :, :].bitcast(F32), ALU.subtract)\
                       .then_inc(low, 1)
                dve.wait_ge(summed, c + 1)
                at_least(dve, turned, c - 1)
                dve.tensor_copy(rows[:, c % 2, :], pd[c % 2][0:B, :]).then_inc(copied, 1)
                dve.wait_ge(turned, c + 1)
                dve.tensor_scalar(val[:, c, :, :], pt[c % 2][:, 0:KD * B].rearrange("p (k b) -> p k b", k=KD),
                                  DEMOD_EPS, None, ALU.add).then_inc(kept, 1)
            count = [0]

            def chain(ins):
                count[0] += 1
                ins.then_inc(step, 1)
                dve.wait_ge(step, count[0])

            dve.wait_ge(kept, 6)
            dve.wait_ge(rooted, 1)
            chain(dve.reciprocal(root[:, :, :, :], root[:, :, :, :]))
            chain(dve.tensor_tensor(tmp[:, :, :, :], root[:, :, :, :], root[:, :, :, :], ALU.mult))
            chain(dve.tensor_tensor(tmp[:, :, :, :], tmp[:, :, :, :], val[:, :, :, :], ALU.mult))
            chain(dve.tensor_scalar(tmp[:, :, :, :], tmp[:, :, :, :], -0.5, 1.5, ALU.mult, ALU.add))
            chain(dve.tensor_tensor(dc[:, :, :, :], tmp[:, :, :, :], root[:, :, :, :], ALU.mult))
            chain(dve.tensor_tensor(dc[:, 0, :, :], dc[:, 0, :, :], dc[:, 1, :, :], ALU.mult))
            chain(dve.tensor_scalar(dc[:, 0, :, :], dc[:, 0, :, :], float(DH) ** -0.5, None, ALU.mult))
            chain(dve.tensor_tensor(dc[:, 2, :, :], dc[:, 2, :, :], cond[:, KD:2 * KD, :], ALU.mult))


def heads_phase(nc, tag, x_in, w, cst, dram, dc, s1, wh, wl):
    with Phase(nc, tag) as ph:
        ident = ph.sb("ident", [P, P])
        ones = ph.sb("ones", [P, P])
        mean_w = ph.sb("mean_w", [P, P])
        mhalf = ph.sb("mhalf", [P, TB])
        xs = ph.sb("xs", [P, KD, TW])
        sq = ph.sb("sq", [P, KD, TW])
        xh = ph.sb("xh", [P, 2, KD, TW], F32R)
        xl = ph.sb("xl", [P, 2, KD, TW], F32R)
        vrow = sq[0:1, 1, :]
        vcol = ph.sb("vcol", [P, TB])
        rcol = ph.sb("rcol", [P, TB])
        diag = sq[:, 0, :].rearrange("p (b s) -> p b s", b=TB)
        qt = ph.sb("qt", [P, TW])
        qh = ph.sb("qh", [P, 2, TW], F32R)
        ql = ph.sb("ql", [P, 2, TW], F32R)
        kh = ph.sb("kh", [P, 2, TB, HG, S], F32R)
        kl = ph.sb("kl", [P, 2, TB, HG, S], F32R)
        vt = ph.sb("vt", [P, 2, TW])
        v = ph.sb("v", [P, 2, TB, DM])
        mx = ph.sb("mx", [P, 2, HG])
        e = ph.sb("e", [P, 4, HG, S])
        pt = ph.sb("pt", [P, 2, HG, S])
        rec = ph.sb("rec", [P, 2 * S])
        o = ph.sb("o", [P, 2, TW])
        ps_s = [ph.ps(f"s{k}") for k in range(2)]
        ps_p = [ph.ps(f"p{k}") for k in range(2)]
        ps_o = [ph.ps(f"o{k}") for k in range(2)]
        ps_t, ps_n = ph.ps("t"), ph.ps("n")
        const, x_ld, xs_ok, mean_mm, xc_ok, sq_ok, var_mm, row_ok, col_mm, col_ok, pow_ok, diag_ok, rs_mm, xn_ok, xh_ok, xl_ok = (
            ph.sem(n) for n in ("const", "x_ld", "xs_ok", "mean_mm", "xc_ok", "sq_ok", "var_mm", "row_ok", "col_mm",
                                "col_ok", "pow_ok", "diag_ok", "rs_mm", "xn_ok", "xh_ok", "xl_ok"))
        pj_mm, qt_ok, qh_ok, ql_ok, kh_ok, kl_ok, vt_ok = (ph.sem(n) for n in (
            "pj_mm", "qt_ok", "qh_ok", "ql_ok", "kh_ok", "kl_ok", "vt_ok"))
        s_mm, mx_ok, sub_ok, exp_ok, tu_mm, tv_mm, pt_ok, v_ok, pv_mm, rec_ok, o_ok = (ph.sem(n) for n in (
            "s_mm", "mx_ok", "sub_ok", "exp_ok", "tu_mm", "tv_mm", "pt_ok", "v_ok", "pv_mm", "rec_ok", "o_ok"))
        vt_st, o_st = ph.sems("vt_st", 2), ph.sems("o_st", 2)
        zeroed, setup = ph.sem("zeroed"), ph.sem("setup")
        block = ph.block()
        x_v = x_in.rearrange("(k p) n -> p k n", p=P)
        v_v = dram["v"].rearrange("(k p) n -> p k n", p=P)
        o_v = dram["o"].rearrange("(k p) n -> p k n", p=P)
        n_pairs = NT // 2
        Q, K, V = range(3)
        CHUNKS = {0: (Q, 1, 0), 1: (K, 1, 0), 2: (V, 2, 0), 4: (Q, 2, 0), 5: (K, 2, 0), 6: (V, 3, 0),
                  8: (Q, 3, 0), 9: (K, 3, 0), 11: (V, 0, 1), 12: (Q, 0, 1), 13: (K, 0, 1), 15: (V, 1, 1)}
        FIRST = [(V, 0), (V, 1), (Q, 0), (K, 0)]
        PER_TILE = len(CHUNKS)
        TURN_LAG, PV_LAG, OUT_LAG = 2, 3, 4

        ORDER = sorted(CHUNKS)

        def chunk_at(u, T, q, last):
            if u not in CHUNKS:
                return None
            kind, m, ahead = CHUNKS[u]
            if ahead and last and q == 1:
                return None
            at = ORDER.index(u)
            before, m_before, ahead_before = CHUNKS[ORDER[at - 2]]
            t_before = T + ahead_before - (at < 2)
            if at < 2 and isinstance(T, int) and T == 0:
                (before, m_before), t_before = FIRST[at - 2], 0
            return kind, m, T + ahead, (q + ahead) % 2, len(FIRST) + PER_TILE * T + at, at % 2, (before, m_before, t_before)

        def first_chunks():
            return [(kind, m, 0, 0, n, n % 2, FIRST[n - 2] + (0,) if n >= 2 else None)
                    for n, (kind, m) in enumerate(FIRST)]

        def lagged(T, q, u, lag, first):
            if u >= lag:
                return (T, q, u - lag) if u - lag < UNITS else None
            return None if first and q == 0 else (T - 1, 1 - q, u - lag + UNITS)

        def v_turns_before(T, u, first, q):
            if first and q == 0 and u == 0:
                return 2
            return KD * T + 1 + (u >= 1) + (u >= 4) + (u >= 8) + (u >= 13)

        def v_turn_at(u, T, q, first, last):
            if u in (4, 8) or (u == 1 and not (first and q == 0)):
                return T, q, (1, 4, 8).index(u) + 1
            if u == 13 and not (last and q == 1):
                return T + 1, 1 - q, 0
            return None

        NORM_START = 8
        SCALE, MEAN, CENTRE, SQUARE, VAR, ROW, COL, COPY, POW, DIAG, SPREAD, NORM, HIGH, LOW = range(14)

        def norm_at(u, steps, T, q, last):
            if u not in steps or (last and (q == 1 or u >= NORM_START)):
                return None
            return (steps[u], T + 2, q) if u >= NORM_START else (steps[u], T + 1, 1 - q)

        DRAIN = range(UNITS, UNITS + OUT_LAG + 2)

        @block.sync
        def _(sp):
            sp.dma_start(ident[:, :], cst["ident"]).then_inc(const, 16)

            def load(T):
                at_least(sp, xl_ok, T)
                sp.dma_start(xs[:, :, :], x_v[:, :, bass.ds(T * TW, TW)]).then_inc(x_ld, 16)

            def store_v(T, m):
                n = KD * T + m
                sp.wait_ge(vt_ok, n + 1)
                sp.dma_start(v_v[:, m, bass.ds(T * TW, TW)], vt[:, m % 2, :]).then_inc(vt_st[m % 2], 16)

            def store_o(T, hg):
                sp.wait_ge(o_ok, 2 * (NG * T + hg + 1))
                hold(sp)
                sp.dma_start(o_v[:, hg, bass.ds(T * TW, TW)], o[:, hg % 2, :]).then_inc(o_st[hg % 2], 16)

            def out_slot(at):
                if at and at[2] % TB == TB - 1:
                    store_o(at[0], at[2] // TB)

            load(0)
            load(1)
            for m in range(2):
                store_v(0, m)

            def body(i, first, last):
                for q in range(2):
                    T = 2 * i + q
                    for u in range(UNITS):
                        if u == NORM_START and not last:
                            load(T + 2)
                        c = chunk_at(u, T, q, last)
                        if c and c[0] == V:
                            store_v(c[2], c[1])
                        out_slot(lagged(T, q, u, OUT_LAG + 1, first))

            pairs(sp, n_pairs, body)
            for u in DRAIN:
                out_slot(lagged(NT - 1, 1, u, OUT_LAG + 1, False))
            for r in range(2):
                sp.wait_ge(vt_st[r], 16 * NT * KD // 2)
                sp.wait_ge(o_st[r], 16 * NT * NG // 2)

        @block.tensor
        def _(pe):
            pe.wait_ge(const, 16)
            pe.wait_ge(setup, 3)

            def chunk(c):
                kind, m, T, q, n, bank, before = c
                if m == 0:
                    pe.wait_ge(xl_ok, T + 1)
                if before:
                    k0, m0, T0 = before
                    done, each = ((qt_ok, 1), (kl_ok, HG), (vt_ok, 1))[k0]
                    pe.wait_ge(done, each * (KD * T0 + m0 + 1))
                for k in range(KD):
                    last = mm3(pe, ps_p[bank][:, :], wh[kind][:, k, m * P:(m + 1) * P], wl[kind][:, k, m * P:(m + 1) * P],
                               xh[:, q, k, :], xl[:, q, k, :], k == 0, k == KD - 1)
                last.then_inc(pj_mm, 1)

            def v_turn(at, unit_turns):
                T, q, m = at
                pe.wait_ge(vt_ok, KD * T + m + 1)
                at_least(pe, pt_ok, unit_turns)
                at_least(pe, v_ok, KD * T + m)
                for b in range(TB):
                    last = pe.transpose(ps_t[:, b * S:(b + 1) * S], vt[:, m % 2, b * S:(b + 1) * S], ident[:, :])
                last.then_inc(tv_mm, 1)

            def norm(step, T, q):
                if step == MEAN:
                    pe.wait_ge(xs_ok, KD * (T + 1))
                    at_least(pe, xn_ok, KD * T)
                    for k in range(KD):
                        last = pe.matmul(ps_n[:, :], mean_w[:, :], xs[:, k, :], start=k == 0, stop=k == KD - 1)
                    last.then_inc(mean_mm, 1)
                elif step == VAR:
                    pe.wait_ge(sq_ok, T + 1)
                    for k in range(KD):
                        last = pe.matmul(ps_n[:, :], mean_w[:, :], sq[:, k, :], start=k == 0, stop=k == KD - 1)
                    last.then_inc(var_mm, 1)
                elif step == COL:
                    pe.wait_ge(row_ok, T + 1)
                    for b in range(TB):
                        last = pe.matmul(ps_n[:, b:b + 1], sq[0:1, 1, b * S:(b + 1) * S], ones[0:1, 0:1], start=True, stop=True)
                    last.then_inc(col_mm, 1)
                else:
                    pe.wait_ge(diag_ok, TB * (T + 1))
                    pe.matmul(ps_n[:, :], ones[:, :], sq[:, 0, :], start=True, stop=True)\
                        .then_inc(rs_mm, 1)

            def scores(T, q, u):
                hg, b = u // TB, u % TB
                g = UNITS * T + u
                if b == 0:
                    pe.wait_ge(ql_ok, NG * T + hg + 1)
                    pe.wait_ge(kl_ok, HG * (NG * T + hg + 1))
                at_least(pe, sub_ok, g - 1)
                mm3(pe, ps_s[u % 2][:, :], qh[:, hg % 2, b * S:(b + 1) * S], ql[:, hg % 2, b * S:(b + 1) * S],
                    kh[:, hg % 2, b, :, :].rearrange("p h s -> p (h s)"),
                    kl[:, hg % 2, b, :, :].rearrange("p h s -> p (h s)"), True, True).then_inc(s_mm, 1)

            def turn(at, v_turns):
                T, q, u = at
                g = UNITS * T + u
                pe.wait_ge(exp_ok, g + 1)
                at_least(pe, pt_ok, g)
                at_least(pe, v_ok, v_turns)
                for h in range(HG):
                    last = pe.transpose(ps_t[:, h * S:(h + 1) * S], e[:, u % 4, h, :], ident[:, :])
                last.then_inc(tu_mm, 1)

            def values(at):
                T, q, u = at
                hg, b = u // TB, u % TB
                g = UNITS * T + u
                pe.wait_ge(pt_ok, g + 1)
                if b == 0:
                    pe.wait_ge(v_ok, KD * T + hg + 1)
                if b % 2 == 0:
                    at_least(pe, o_ok, UNITS // 2 * T + u // 2 - 1)
                bank = ps_o[(u // 2) % 2]
                c = (b % 2) * S
                for h in range(HG):
                    pe.matmul(bank[h * DH:(h + 1) * DH, c:c + S], v[:, q, b, (hg * HG + h) * DH:(hg * HG + h + 1) * DH],
                              pt[:, u % 2, h, :], start=True, stop=True)
                for h in range(HG):
                    last = pe.matmul(bank[h * DH:(h + 1) * DH, 2 * S + c:3 * S + c], ones[:, 0:DH],
                                     pt[:, u % 2, h, :], start=True, stop=True)
                last.then_inc(pv_mm, 1)

            for step in (MEAN, VAR, COL, SPREAD):
                norm(step, 0, 0)
            norm(MEAN, 1, 1)
            for c in first_chunks():
                chunk(c)
                if c[0] == V and c[1]:
                    v_turn((0, 0, c[1] - 1), 0)
                elif c[0] == Q:
                    v_turn((0, 0, 1), 0)

            def slot(T, q, u, first, last):
                if u < UNITS:
                    scores(T, q, u)
                    vt_at = v_turn_at(u, T, q, first, last)
                    if vt_at:
                        v_turn(vt_at, UNITS * T + u - TURN_LAG)
                    c = chunk_at(u, T, q, last)
                    if c:
                        chunk(c)
                    at = norm_at(u, {13: MEAN, 0: VAR, 3: COL, 5: SPREAD}, T, q, last)
                    if at:
                        norm(*at)
                at = lagged(T, q, u, TURN_LAG, first)
                turns = v_turns_before(T, u, first, q) if not (last and q == 1 and u >= 13) else KD * T + 4
                if at:
                    turn(at, turns)
                at = lagged(T, q, u, PV_LAG, first)
                if at:
                    values(at)

            def body(i, first, last):
                for q in range(2):
                    for u in range(UNITS):
                        slot(2 * i + q, q, u, first, last)

            pairs(pe, n_pairs, body)
            for u in DRAIN:
                slot(NT - 1, 1, u, False, True)

        @block.scalar
        def _(act):
            def chunk(c):
                kind, m, T, q, n, bank, before = c
                if kind == Q:
                    act.wait_ge(qt_ok, NG * T + m + 1)
                    at_least(act, s_mm, UNITS * T + TB * (m - 1))
                    act.activation(qh[:, m % 2, :], qt[:, :], ACT.Copy).then_inc(qh_ok, 1)
                elif kind == K:
                    act.wait_ge(pj_mm, n + 1)
                    at_least(act, s_mm, UNITS * T + TB * (m - 1))
                    for h in range(HG):
                        r = slice(h * DH, (h + 1) * DH)
                        last = act.activation(kh[r, m % 2, :, h, :], ps_p[bank][r, :].rearrange("p (b s) -> p b s", b=TB),
                                              ACT.Copy)
                        last.then_inc(kh_ok, 1)

            def keep_v(at):
                T, q, m = at
                act.wait_ge(tv_mm, KD * T + m + 1)
                at_least(act, pv_mm, UNITS * (T - 1))
                act.activation(v[:, q, :, m * P:(m + 1) * P], ps_t[:, :].rearrange("p (b s) -> p b s", b=TB), ACT.Copy)\
                    .then_inc(v_ok, 1)

            def norm(step, T, q):
                if step == SQUARE:
                    act.wait_ge(xc_ok, KD * (T + 1))
                    at_least(act, rs_mm, T)
                    act.activation(sq[:, :, :], xs[:, :, :], ACT.Square).then_inc(sq_ok, 1)
                else:
                    act.wait_ge(xn_ok, KD * (T + 1))
                    at_least(act, pj_mm, len(FIRST) + PER_TILE * (T - 2) + ORDER.index(9) + 1)
                    act.activation(xh[:, q, :, :], xs[:, :, :], ACT.Copy).then_inc(xh_ok, 1)

            act.wait_ge(zeroed, 2)
            norm(SQUARE, 0, 0)
            norm(HIGH, 0, 0)
            norm(SQUARE, 1, 1)
            for c in first_chunks():
                chunk(c)
                if c[0] == V and c[1]:
                    keep_v((0, 0, c[1] - 1))
                elif c[0] == Q:
                    keep_v((0, 0, 1))

            def slot(T, q, u, first, last):
                if u < UNITS:
                    vt_at = v_turn_at(u, T, q, first, last)
                    if vt_at:
                        keep_v(vt_at)
                    g = UNITS * T + u
                    act.wait_ge(sub_ok, g + 1)
                    act.activation(e[:, u % 4, :, :], e[:, u % 4, :, :], ACT.Exp).then_inc(exp_ok, 1)
                    c = chunk_at(u, T, q, last)
                    if c:
                        chunk(c)
                at = lagged(T, q, u, TURN_LAG, first)
                if at:
                    g = UNITS * at[0] + at[2]
                    act.wait_ge(tu_mm, g + 1)
                    at_least(act, pv_mm, g - 1)
                    act.activation(pt[:, at[2] % 2, :, :], ps_t[:, :].rearrange("p (h s) -> p h s", h=HG), ACT.Copy)\
                        .then_inc(pt_ok, 1)
                at = norm_at(u, {15: SQUARE, 7: HIGH}, T, q, last)
                if at:
                    norm(*at)

            def body(i, first, last):
                for q in range(2):
                    for u in range(UNITS):
                        slot(2 * i + q, q, u, first, last)

            pairs(act, n_pairs, body)
            for u in DRAIN:
                slot(NT - 1, 1, u, False, True)

        @block.vector
        def _(dve):
            dve.memset(kh[:, :, :, :, :].bitcast(F32), 0.0).then_inc(zeroed, 1)
            dve.memset(kl[:, :, :, :, :].bitcast(F32), 0.0).then_inc(zeroed, 1)
            dve.memset(ones[:, :], 1.0).then_inc(setup, 1)
            dve.memset(mean_w[:, :], 1.0 / DM).then_inc(setup, 1)
            dve.memset(mhalf[:, :], -0.5).then_inc(setup, 1)
            dve.wait_ge(setup, 3)
            dve.wait_ge(const, 16)
            dve.wait_ge(zeroed, 2)

            def per_batch(c, m, T):
                return dc[:, c, m, bass.ds(T * TB, TB)].unsqueeze(2).to_broadcast([P, TB, S])

            def chunk(c):
                kind, m, T, q, n, bank, before = c
                src = ps_p[bank]
                if kind == K:
                    at_least(dve, s_mm, UNITS * T + TB * (m - 1))
                    for h in range(HG):
                        dve.wait_ge(kh_ok, HG * (NG * T + m) + h + 1)
                        r = slice(h * DH, (h + 1) * DH)
                        last = dve.tensor_tensor(kl[r, m % 2, :, h, :], src[r, :].rearrange("p (b s) -> p b s", b=TB),
                                                 kh[r, m % 2, :, h, :].bitcast(F32), ALU.subtract)
                        last.then_inc(kl_ok, 1)
                else:
                    dve.wait_ge(pj_mm, n + 1)
                    if kind == Q:
                        at_least(dve, ql_ok, NG * T + m)
                        dve.tensor_tensor(qt[:, :].rearrange("p (b s) -> p b s", b=TB),
                                          src[:, :].rearrange("p (b s) -> p b s", b=TB), per_batch(0, m, T), ALU.mult)\
                            .then_inc(qt_ok, 1)
                    else:
                        at_least(dve, vt_st[m % 2], 16 * (KD // 2 * T + m // 2))
                        at_least(dve, tv_mm, KD * T + m - 1)
                        dve.tensor_tensor(vt[:, m % 2, :].rearrange("p (b s) -> p b s", b=TB),
                                          src[:, :].rearrange("p (b s) -> p b s", b=TB), per_batch(2, m, T), ALU.mult)\
                            .then_inc(vt_ok, 1)

            def norm(step, T, q):
                if step == CENTRE:
                    dve.wait_ge(mean_mm, T + 1)
                    for k in range(KD):
                        dve.tensor_tensor(xs[:, k, :], xs[:, k, :], ps_n[:, :], ALU.subtract).then_inc(xc_ok, 1)
                elif step == ROW:
                    dve.wait_ge(var_mm, T + 1)
                    dve.tensor_scalar(vrow, ps_n[0:1, :], LN_EPS, None, ALU.add).then_inc(row_ok, 1)
                elif step == COPY:
                    dve.wait_ge(col_mm, T + 1)
                    dve.tensor_copy(vcol[:, :], ps_n[:, 0:TB]).then_inc(col_ok, 1)
                elif step == DIAG:
                    dve.wait_ge(pow_ok, T + 1)
                    for b in range(TB):
                        dve.tensor_scalar(diag[:, b, :], ident[:, :], rcol[:, b:b + 1], None, ALU.mult).then_inc(diag_ok, 1)
                else:
                    dve.wait_ge(rs_mm, T + 1)
                    dve.wait_ge(xc_ok, KD * (T + 1))
                    dve.wait_ge(sq_ok, T + 1)
                    for k in range(KD):
                        dve.tensor_tensor(xs[:, k, :], xs[:, k, :], ps_n[:, :], ALU.mult).then_inc(xn_ok, 1)

            for step in (CENTRE, ROW, COPY, DIAG, NORM):
                norm(step, 0, 0)
            norm(CENTRE, 1, 1)
            for c in first_chunks():
                chunk(c)

            def softmax(T, q, u):
                g = UNITS * T + u
                shape = [P, HG, S]
                src = ps_s[u % 2][:, :].rearrange("p (h s) -> p h s", h=HG)
                dve.wait_ge(s_mm, g + 1)
                at_least(dve, sub_ok, g - 1)
                dve.reduce_max(mx[:, u % 2, :], src, AX.X).then_inc(mx_ok, 1)
                dve.wait_ge(mx_ok, g + 1)
                at_least(dve, tu_mm, g - 3)
                dve.tensor_tensor(e[:, u % 4, :, :], src, mx[:, u % 2, :].unsqueeze(2).to_broadcast(shape), ALU.subtract)\
                    .then_inc(sub_ok, 1)

            def finish(at):
                T, q, u = at
                hg, b = u // TB, u % TB
                pair = UNITS // 2 * T + u // 2
                dve.wait_ge(pv_mm, UNITS * T + u + 1)
                bank = ps_o[(u // 2) % 2]
                at_least(dve, o_ok, pair)
                dve.reciprocal(rec[:, :], bank[:, 2 * S:4 * S]).then_inc(rec_ok, 1)
                dve.wait_ge(rec_ok, pair + 1)
                if b == 1:
                    at_least(dve, o_st[hg % 2], 16 * (NG // 2 * T + hg // 2))
                dve.tensor_tensor(o[:, hg % 2, (b - 1) * S:(b + 1) * S], bank[:, 0:2 * S], rec[:, :], ALU.mult)\
                    .then_inc(o_ok, 1)

            def slot(T, q, u, first, last):
                if u < UNITS:
                    softmax(T, q, u)
                    at = norm_at(u, {2: ROW, 3: COPY, 4: DIAG}, T, q, last)
                    if at:
                        norm(*at)
                    c = chunk_at(u, T, q, last)
                    if c:
                        chunk(c)
                at = lagged(T, q, u, OUT_LAG, first)
                if at and at[2] % 2:
                    finish(at)
                at = norm_at(u, {14: CENTRE, 6: NORM}, T, q, last)
                if at:
                    norm(*at)

            def body(i, first, last):
                for q in range(2):
                    for u in range(UNITS):
                        slot(2 * i + q, q, u, first, last)

            pairs(dve, n_pairs, body)
            for u in DRAIN:
                slot(NT - 1, 1, u, False, True)

        @block.gpsimd
        def _(pool):
            pool.wait_ge(setup, 3)

            def norm(step, T, q):
                if step == SCALE:
                    pool.wait_ge(x_ld, 16 * (T + 1))
                    for k in range(KD):
                        scale = s1[:, k, bass.ds(T * TB, TB)].unsqueeze(2).to_broadcast([P, TB, S])
                        view = xs[:, k, :].rearrange("p (b s) -> p b s", b=TB)
                        pool.tensor_tensor(view, view, scale, ALU.mult).then_inc(xs_ok, 1)
                elif step == POW:
                    pool.wait_ge(col_ok, T + 1)
                    at_least(pool, diag_ok, TB * T)
                    pool.tensor_tensor(rcol[:, :], vcol[:, :], mhalf[:, :], ALU.pow).then_inc(pow_ok, 1)
                else:
                    pool.wait_ge(xh_ok, T + 1)
                    pool.tensor_tensor(xl[:, q, :, :], xs[:, :, :], xh[:, q, :, :].bitcast(F32), ALU.subtract)\
                        .then_inc(xl_ok, 1)

            def chunk(c):
                kind, m, T, q, n, bank, before = c
                if kind == Q:
                    pool.wait_ge(qh_ok, NG * T + m + 1)
                    pool.tensor_tensor(ql[:, m % 2, :], qt[:, :], qh[:, m % 2, :].bitcast(F32), ALU.subtract)\
                        .then_inc(ql_ok, 1)

            for step in (SCALE, POW, LOW):
                norm(step, 0, 0)
            norm(SCALE, 1, 1)
            for c in first_chunks():
                chunk(c)

            def body(i, first, last):
                for q in range(2):
                    T = 2 * i + q
                    for u in range(UNITS):
                        c = chunk_at(u, T, q, last)
                        if c:
                            chunk(c)
                        at = norm_at(u, {11: SCALE, 3: POW, 7: LOW}, T, q, last)
                        if at:
                            norm(*at)

            pairs(pool, n_pairs, body)


def mix_phase(nc, tag, x_in, x_out, w, cst, dram, dc, wh, wl):
    with Phase(nc, tag) as ph:
        wh, wl = wh + [ph.sb("uh", [P, KD, DM], F32R)], wl + [ph.sb("ul", [P, KD, DM], F32R)]
        view = w["uT"].rearrange("(k p) n -> p k n", p=P)
        split_weights(nc, tag + "w", [(view[:, k, :], wh[1][:, k, :], wl[1][:, k, :]) for k in range(KD)])
        xt = ph.sb("xt", [P, 2, KD, TW])
        src = ph.sb("src", [P, 2, KD, TW])
        hi = ph.sb("hi", [P, 2, 2, KD, TW], F32R)
        lo = ph.sb("lo", [P, 2, 2, KD, TW], F32R)
        t = ph.sb("t", [P, 2, TW])
        ps = [ph.ps(f"ps{k}") for k in range(4)]
        s_ld, x_ld, x_st = ph.sems("s_ld", 2), ph.sems("x_ld", 2), ph.sems("x_st", 2)
        high, low, mm, scaled, added = (ph.sem(n) for n in ("high", "low", "mm", "scaled", "added"))
        block = ph.block()
        x_v, y_v, v_v, o_v = (a.rearrange("(k p) n -> p k n", p=P) for a in (x_in, x_out, dram["v"], dram["o"]))
        n_pairs = NT // 2
        NC = 2 * KD

        @block.sync
        def _(sp):
            def load(T, q, uses):
                cols = bass.ds(T * TW, TW)
                for c, a in enumerate((o_v, v_v)):
                    at_least(sp, low, 2 * (T - 1) + c + 1)
                    sp.dma_start(src[:, c, :, :], a[:, :, cols]).then_inc(s_ld[c], 16)
                at_least(sp, x_st[q], 16 * uses)
                sp.dma_start(xt[:, q, :, :], x_v[:, :, cols]).then_inc(x_ld[q], 16)

            def store(T, q):
                sp.wait_ge(added, NC * (T + 1))
                sp.dma_start(y_v[:, :, bass.ds(T * TW, TW)], xt[:, q, :, :]).then_inc(x_st[q], 16)

            def body(i, first, last):
                for q in range(2):
                    T = 2 * i + q
                    if first and q == 0:
                        load(0, 0, 0)
                    if not (first and q == 0):
                        store(T - 1, 1 - q)
                    if not (last and q == 1):
                        load(T + 1, 1 - q, i + q)

            pairs(sp, n_pairs, body)
            store(NT - 1, 1)
            for q in range(2):
                sp.wait_ge(x_st[q], 16 * n_pairs)

        @block.scalar
        def _(act):
            def split(T, q):
                for c in range(2):
                    act.wait_ge(s_ld[c], 16 * (T + 1))
                    at_least(act, mm, NC * (T - 1))
                    act.activation(hi[:, q, c, :, :], src[:, c, :, :], ACT.Copy).then_inc(high, 1)

            def body(i, first, last):
                for q in range(2):
                    split(2 * i + q, q)

            pairs(act, n_pairs, body)

        @block.tensor
        def _(pe):
            def body(i, first, last):
                for q in range(2):
                    T = 2 * i + q
                    for m in range(KD):
                        for c in range(2):
                            n = NC * T + 2 * m + c
                            if m == 0:
                                pe.wait_ge(low, 2 * T + c + 1)
                            at_least(pe, scaled, n - 3)
                            for k in range(KD):
                                last_mm = mm3(pe, ps[(2 * m + c) % 4][:, :], wh[c][:, k, m * P:(m + 1) * P],
                                              wl[c][:, k, m * P:(m + 1) * P], hi[:, q, c, k, :], lo[:, q, c, k, :],
                                              k == 0, k == KD - 1)
                            last_mm.then_inc(mm, 1)

            pairs(pe, n_pairs, body)

        @block.vector
        def _(dve):
            def split(T, q):
                for c in range(2):
                    dve.wait_ge(high, 2 * T + c + 1)
                    dve.tensor_tensor(lo[:, q, c, :, :], src[:, c, :, :], hi[:, q, c, :, :].bitcast(F32), ALU.subtract)\
                        .then_inc(low, 1)

            def body(i, first, last):
                for q in range(2):
                    T = 2 * i + q
                    if first and q == 0:
                        split(0, 0)
                    for m in range(KD):
                        for c in range(2):
                            n = NC * T + 2 * m + c
                            dve.wait_ge(mm, n + 1)
                            at_least(dve, added, n - 1)
                            scale = dc[:, 3 + c, m, bass.ds(T * TB, TB)].unsqueeze(2).to_broadcast([P, TB, S])
                            dve.tensor_tensor(t[:, c, :].rearrange("p (b s) -> p b s", b=TB),
                                              ps[(2 * m + c) % 4][:, :].rearrange("p (b s) -> p b s", b=TB),
                                              scale, ALU.mult).then_inc(scaled, 1)
                        if m == 1 and not (last and q == 1):
                            split(T + 1, 1 - q)

            pairs(dve, n_pairs, body)

        @block.gpsimd
        def _(pool):
            def body(i, first, last):
                for q in range(2):
                    T = 2 * i + q
                    pool.wait_ge(x_ld[q], 16 * (i + 1))
                    for m in range(KD):
                        for c in range(2):
                            n = NC * T + 2 * m + c
                            pool.wait_ge(scaled, n + 1)
                            at_least(pool, added, n)
                            pool.tensor_tensor(xt[:, q, m, :], xt[:, q, m, :], t[:, c, :], ALU.add).then_inc(added, 1)

            pairs(pool, n_pairs, body)


def build(nc, a, out, layers="0123"):
    def scratch(name, shape, dt=F32):
        return nc.dram_tensor(name, shape, dt, kind="Internal").ap()

    dram = dict(gate=scratch("gate_s", (DI, TOK)), xhl=scratch("xhl_s", (S, 2, B, DI)),
                dx=scratch("dx_s", (S, B, DI)), y=scratch("y_s", (S, B, DI)),
                v=scratch("v_s", (DM, TOK)), o=scratch("o_s", (DM, TOK)))
    cst = dict(ident=a["ident"], pick=a["pick"], ymask=a["ymask"])

    def weights(layer):
        w = {k[3:]: v for k, v in a.items() if k.startswith(f"L{layer}_")}
        w["tembT"] = w["condT"] = a["condT"]
        w["ident"] = a["ident"]
        return w

    x = a["xT"]
    for n, layer in enumerate(layers):
        y = out if n == len(layers) - 1 else scratch(f"x{layer}_s", (DM, TOK))
        (scan_layer if layer in "03" else attention_layer)(nc, f"l{layer}", x, y, weights(layer), cst, dram)
        x = y


def kernel(**inputs):
    import numpy as np
    import concourse.bacc as bacc
    from concourse.bass_utils import run_bass_kernel_spmd

    def columns(v):
        return np.ascontiguousarray(v.reshape(-1, P).T)

    a = {k: np.asarray(v) for k, v in inputs.items()}
    arrays = {"xT": a["x"].reshape(TOK, DM).T, "condT": a["cond_2048"].T}
    for layer in (0, 3):
        w = {k.split("cond_", 1)[1]: v for k, v in a.items() if k.startswith(f"L{layer}_cond_")}
        arrays.update({f"L{layer}_{k}": v for k, v in dict(
            W_inT=w["W_in"].T, W_conv=w["W_conv"], b_convT=columns(w["b_conv"]), ln_gT=columns(w["ln_g"]),
            ln_bT=columns(w["ln_b"]), ln_g=w["ln_g"], ln_b=w["ln_b"], D=w["D"], W_xprojT=w["W_xproj"].T,
            W_xproj=w["W_xproj"], W_dtT=w["W_dt"].T, b_dt=w["b_dt"], A_log=w["A_log"], W_outT=w["W_out"].T).items()})
    for layer in (1, 2):
        for k in "qkvwu":
            arrays[f"L{layer}_{k}T"] = a[f"L{layer}_cond_{k}_weight"].T
    arrays["ident"] = np.eye(P, dtype=np.float32)
    pick = np.zeros((2, 2, GJ, GB, 2, GJ, GB, NS), np.float32)
    ymask = np.zeros((GB, NS, TS, TS, GB), np.float32)
    for b in range(GB):
        for j in range(GJ):
            for t in range(2):
                pick[t, :, j, b, t, j, b, :] = 1.0
        for t in range(TS):
            ymask[b, :, t, t, b] = 1.0
    arrays["pick"] = pick.reshape(P, 2, GJ, P)
    arrays["ymask"] = ymask.reshape(P, TS, TS * GB)
    arrays = {k: np.ascontiguousarray(v) for k, v in arrays.items()}
    arrays = {k: v for k, v in arrays.items() if not k.startswith("L") or k[1] in LAYERS}

    nc = bacc.Bacc("TRN2", target_bir_lowering=False, num_devices=1)
    aps = {k: nc.dram_tensor(k, v.shape, F32, kind="ExternalInput").ap() for k, v in arrays.items()}
    out = nc.dram_tensor("outT", (DM, TOK), F32, kind="ExternalOutput").ap()
    build(nc, aps, out, LAYERS)
    r = run_bass_kernel_spmd(nc, [arrays], core_ids=[0])
    return np.ascontiguousarray(r.results[0]["outT"].T).reshape(B, S, DM)
LAYERS = "0123"
```
